# Optimizing a Trainium2 kernel written in Bass

```python
import numpy as np
import jax
import jax.numpy as jnp

def _softmax(x, axis=-1):
    return jax.nn.softmax(x, axis=axis)

def _gelu(x):
    return jax.nn.gelu(x, approximate=True)

def _silu(x):
    return jax.nn.silu(x)

def _sigmoid(x):
    return jax.nn.sigmoid(x)

def _layernorm(x, axis=-1, eps=1e-05):
    m = jnp.mean(x, axis=axis, keepdims=True)
    v = jnp.var(x, axis=axis, keepdims=True)
    return (x - m) / jnp.sqrt(v + eps)

def _scatter_add(tgt, idx, src, axis=0):
    return tgt.at[idx].add(src)

def _segment_sum(src, seg, n):
    return jax.ops.segment_sum(src, seg, n)
kernel_name = 'mk_adj_ffn_d1_adj_r2_e4d03a'

def setup_inputs(seed: int=0):
    np.random.seed(seed)
    _w = jnp.asarray

    def _rec_inputs():
        import jax
        import jax.numpy as jnp
        _gk = jax.random.key(seed)
        x = 7.22e-05 + 1 * jax.random.normal(jax.random.fold_in(_gk, 1), (16, 512, 256), jnp.float32)
        _a = jax.random.bernoulli(jax.random.fold_in(_gk, 2), 0.03125, (16, 512, 512))
        _a = jnp.logical_or(_a, jnp.swapaxes(_a, -1, -2))
        _a = jnp.logical_or(_a, jnp.eye(512, dtype=bool))
        _af = _a.astype(jnp.float32)
        _af = _af * jax.random.uniform(jax.random.fold_in(_gk, 3), (16, 512, 512), jnp.float32, 0.05, 1)
        adj = _af
        return (x, adj)
    x, adj = _rec_inputs()

    def _L0_gnn_setup():
        import jax, jax.numpy as jnp
        import numpy as np
        EPS_LN = 1e-05

        def hypergraph_conv(x, adj, W, b):
            N, C, _ = adj.shape
            H = (adj != 0).astype(x.dtype)
            w = adj.reshape(N, -1)[:, :C]
            xw = jnp.einsum('ncd,hd->nch', x, W)
            Dn = jnp.einsum('nce,ne->nc', H, w)
            Dn = jnp.where(Dn > 0, 1.0 / Dn, 0.0)
            Be = H.sum(axis=1)
            Be = jnp.where(Be > 0, 1.0 / Be, 0.0)
            m = Be[:, :, None] * jnp.einsum('nce,nch->neh', H, xw)
            out = Dn[:, :, None] * jnp.einsum('nce,neh->nch', H, m)
            return out + b

        def layer_norm(x, g, b):
            mu = jnp.mean(x, axis=-1, keepdims=True)
            var = jnp.var(x, axis=-1, keepdims=True)
            return (x - mu) * jax.lax.rsqrt(var + EPS_LN) * g + b
        key = jax.random.key(seed)
        ks = jax.random.split(key, 4)
        N, C, Din, Dh, Dout = (16, 512, 256, 512, 256)
        x = jax.random.normal(ks[0], (N, C, Din), dtype=jnp.float32)
        adj = jax.random.uniform(ks[1], (N, C, C), dtype=jnp.float32, minval=0.1, maxval=1.0)
        W1 = jax.random.normal(ks[2], (Dh, Din), dtype=jnp.float32) * (1.0 / np.sqrt(Din))
        b1 = jnp.zeros((Dh,), dtype=jnp.float32)
        gamma = jnp.ones((Dh,), dtype=jnp.float32)
        beta = jnp.zeros((Dh,), dtype=jnp.float32)
        W2 = jax.random.normal(ks[3], (Dout, Dh), dtype=jnp.float32) * (1.0 / np.sqrt(Dh))
        b2 = jnp.zeros((Dout,), dtype=jnp.float32)
        return {'x': x, 'adj': adj, 'W1': W1, 'b1': b1, 'gamma': gamma, 'beta': beta, 'W2': W2, 'b2': b2}
    _L0_gnn_all = _L0_gnn_setup()
    _L0_gnn_in = {k: v for k, v in _L0_gnn_all.items() if k in ('W1', 'b1', 'gamma', 'beta', 'W2', 'b2')}
    del _L0_gnn_all

    def _L0_ffn_setup():
        import jax, jax.numpy as jnp
        import numpy as np
        FP8_MAX = 448.0
        K, N = (256, 256)
        key = jax.random.key(seed)
        kx, kw = jax.random.split(key)
        x = jax.random.normal(kx, (8, 4096, K), dtype=jnp.float32)
        weight = jax.random.normal(kw, (K, N), dtype=jnp.float32) * 0.02
        return {'x': x, 'weight': weight}
    _L0_ffn_all = _L0_ffn_setup()
    _L0_ffn_in = {k: v for k, v in _L0_ffn_all.items() if k in ('weight',)}
    del _L0_ffn_all
    return {'x': x, 'adj': adj, 'L0_gnn_W1': _L0_gnn_in['W1'], 'L0_gnn_b1': _L0_gnn_in['b1'], 'L0_gnn_gamma': _L0_gnn_in['gamma'], 'L0_gnn_beta': _L0_gnn_in['beta'], 'L0_gnn_W2': _L0_gnn_in['W2'], 'L0_gnn_b2': _L0_gnn_in['b2'], 'L0_ffn_weight': _L0_ffn_in['weight']}

def reference(x, adj, L0_gnn_W1, L0_gnn_b1, L0_gnn_gamma, L0_gnn_beta, L0_gnn_W2, L0_gnn_b2, L0_ffn_weight):
    import jax
    import jax.numpy as jnp

    def _L0_gnn_ref(x, adj, W1, b1, gamma, beta, W2, b2):
        import jax, jax.numpy as jnp
        import numpy as np
        EPS_LN = 1e-05

        def hypergraph_conv(x, adj, W, b):
            N, C, _ = adj.shape
            H = (adj != 0).astype(x.dtype)
            w = adj.reshape(N, -1)[:, :C]
            xw = jnp.einsum('ncd,hd->nch', x, W)
            Dn = jnp.einsum('nce,ne->nc', H, w)
            Dn = jnp.where(Dn > 0, 1.0 / Dn, 0.0)
            Be = H.sum(axis=1)
            Be = jnp.where(Be > 0, 1.0 / Be, 0.0)
            m = Be[:, :, None] * jnp.einsum('nce,nch->neh', H, xw)
            out = Dn[:, :, None] * jnp.einsum('nce,neh->nch', H, m)
            return out + b

        def layer_norm(x, g, b):
            mu = jnp.mean(x, axis=-1, keepdims=True)
            var = jnp.var(x, axis=-1, keepdims=True)
            return (x - mu) * jax.lax.rsqrt(var + EPS_LN) * g + b
        h = jax.nn.relu(hypergraph_conv(x, adj, W1, b1))
        h = layer_norm(h, gamma, beta)
        y = hypergraph_conv(h, adj, W2, b2)
        return y + x

    def _L0_ffn_ref(x, weight):
        import jax, jax.numpy as jnp
        import numpy as np
        FP8_MAX = 448.0
        K, N = (256, 256)
        B, S, _ = x.shape
        x2d = x.reshape(-1, K)
        x_amax = jnp.max(jnp.abs(x2d))
        x_scale = FP8_MAX / jnp.maximum(x_amax, 1e-12)
        x_fp8 = jnp.clip(x2d * x_scale, -FP8_MAX, FP8_MAX).astype(jnp.float8_e4m3fn)
        w_amax = jnp.max(jnp.abs(weight))
        w_scale = FP8_MAX / jnp.maximum(w_amax, 1e-12)
        w_fp8 = jnp.clip(weight.T * w_scale, -FP8_MAX, FP8_MAX).astype(jnp.float8_e4m3fn)
        res = jnp.matmul(x_fp8.astype(jnp.float32), w_fp8.astype(jnp.float32).T)
        out = res * (1.0 / x_scale * (1.0 / w_scale))
        return out.reshape(B, S, N).astype(x.dtype)
    x = x + _L0_gnn_ref(_layernorm(x, axis=-1), adj, L0_gnn_W1, L0_gnn_b1, L0_gnn_gamma, L0_gnn_beta, L0_gnn_W2, L0_gnn_b2)
    x = x + _L0_ffn_ref(_layernorm(x, axis=-1), L0_ffn_weight)
    return x

_drawn_inputs = setup_inputs


def setup_inputs(seed=0):
    import zlib

    import numpy as np

    out = dict(_drawn_inputs(seed))
    spreads = {'L0_gnn_b1': (0.0, 0.1),
     'L0_gnn_gamma': (1.0, 0.2),
     'L0_gnn_beta': (0.0, 0.1),
     'L0_gnn_b2': (0.0, 2.0)}
    factors = {'L0_ffn_weight': 8.0}
    for name, (base, spread) in spreads.items():
        noise = np.random.default_rng([zlib.crc32(name.encode()), seed]).standard_normal(out[name].shape)
        drawn = base * np.exp(spread * noise) if base else spread * noise
        out[name] = jnp.asarray(drawn.astype(out[name].dtype))
    for name, factor in factors.items():
        out[name] = (out[name] * factor).astype(out[name].dtype)
    return out
```

```python
import concourse.bass as bass
from concourse import mybir
from concourse.alu_op_type import AluOpType as ALU
from contextlib import ExitStack


def adjacency_gnn_then_fp8_ffn(nc, x, adj, W1, b1, gamma, beta, W2, b2, ffn_w, out):
    FP32, FP16, BF16, U32 = mybir.dt.float32, mybir.dt.float16, mybir.dt.bfloat16, mybir.dt.uint32
    ACT = mybir.ActivationFunctionType
    AX = mybir.AxisListType
    ALL_REDUCE_MAX = bass.bass_isa.ReduceOp.max

    PART = 128
    G, C, D = x.shape
    F = W1.shape[0]
    TILES = C // PART
    DT = D // PART
    FT = F // PART
    assert (TILES, DT, FT) == (4, 2, 4) and G % 2 == 0 and G >= 6 and W2.shape == (D, F) and ffn_w.shape == (D, D)
    PAIRS = TILES // 2
    EPS = 1e-5
    FP8_MAX = 448.0
    AMAX_FLOOR = 1e-12
    SMALLEST = 1.2e-38
    M_SCALE = 64.0
    Z_DOWN = 1.0 / 16.0
    Z_SCALE = M_SCALE * Z_DOWN
    W_SCALE = 256.0
    X_DOWN = 1.0 / 16.0
    X_SCALE = W_SCALE * X_DOWN
    EXPONENT = 0x7F800000
    ROUND_FLOOR = 1.5 * 2.0 ** -6
    ROUND_SCALE = float(2 ** 20 - 1)
    W_PAD = 4
    U_STRIDE = D + 2

    x_dram = x.rearrange("g (p k) d -> g p k d", k=TILES)
    adj_dram = adj.rearrange("g (p k) e -> g p k e", k=TILES)
    out_dram = out.rearrange("g (p k) d -> g p k d", k=TILES)
    edge_w_dram = adj[:, 0, :]

    with ExitStack() as ctx:
        def sb(name, shape, dt):
            return ctx.enter_context(nc.sbuf_tensor(name, shape, dt))

        rows = sb("rows", [PART, 240], FP32)
        taken = [0]

        def small(*shape):
            size = 1
            for s in shape:
                size *= s
            at, taken[0] = taken[0], taken[0] + size
            part = rows[:, at:at + size]
            return part if len(shape) == 1 else part.rearrange("p (a b) -> p a b", b=shape[1])

        def sem(name):
            return ctx.enter_context(nc.semaphore(name))

        x1 = sb("x1", [PART, G, TILES, D], FP32)
        vT = sb("vT", [PART, G, DT, C], FP32)
        w1_hi = sb("w1_hi", [PART, DT, F], FP16)
        w1_lo = sb("w1_lo", [PART, DT, F], FP16)
        w2_hi = sb("w2_hi", [PART, FT, D], FP16)
        w2_lo = sb("w2_lo", [PART, FT, D], FP16)
        wq = sb("wq", [PART, DT, D], BF16)
        b1_all = sb("b1_all", [PART, F], FP32)
        b2_all = sb("b2_all", [PART, D], FP32)
        gamma_col = sb("gamma_col", [PART, FT], FP32)
        beta_col = sb("beta_col", [PART, FT], FP32)
        ident = sb("ident", [PART, PART], FP32)
        ident16 = sb("ident16", [PART, PART], FP16)
        bias_row = sb("bias_row", [PART, PAIRS, D], FP16)
        bias_lhs = sb("bias_lhs", [PART, PART], FP16)
        edge_w = sb("edge_w", [PART, TILES, G, W_PAD], BF16)
        edge_w_now = sb("edge_w_now", [PART, TILES, W_PAD], BF16)
        adj_in = sb("adj_in", [PART, TILES, C], FP32)
        H = [sb(f"H{p}", [PART, TILES, C], FP16) for p in range(2)]
        HT = [sb(f"HT{p}", [PART, TILES, C], FP16) for p in range(2)]
        u = sb("u", [PART, TILES, D], FP32)
        u_hi = sb("u_hi", [PART, TILES, U_STRIDE], FP16)
        u_lo = sb("u_lo", [PART, TILES, D], FP16)
        m_hi = sb("m_hi", [PART, TILES, D], FP16)
        m_lo = sb("m_lo", [PART, TILES, D], FP16)
        z_hi = sb("z_hi", [PART, DT, C], FP16)
        z_lo = sb("z_lo", [PART, DT, C], FP16)
        h = sb("h", [PART, TILES, F], FP32)
        squares = [part[:, k, :].bitcast(BF16) for part in (z_hi, z_lo) for k in range(DT)]
        hT_hi = sb("hT_hi", [PART, TILES, F], FP16)
        hT_lo = sb("hT_lo", [PART, TILES, F], FP16)
        xw_hi = sb("xw_hi", [PART, TILES, D], FP16)
        xw_lo = sb("xw_lo", [PART, TILES, D], FP16)
        v = sb("v", [PART, TILES, D], FP32)
        minus_half = small(TILES)
        eps_col = small(TILES)
        one_by_f = small(TILES)
        pool_gate = small(TILES)
        dve_gate = small(4)
        x_six = small(TILES, 6)
        x_mv = small(TILES, 2)
        x_var = small(TILES)
        x_rstd = small(TILES)
        count64 = small(TILES)
        binv64 = small(TILES)
        binv = [small(TILES) for p in range(2)]
        deg = small(TILES)
        deg_pos = small(TILES)
        deg_safe = small(TILES)
        deg_inv = small(TILES)
        dinv = small(TILES)
        dinv1 = small(TILES)
        dinv2 = [small(TILES) for p in range(2)]
        h_sum = small(TILES)
        h_neg_mean = small(TILES)
        h_sq = small(TILES)
        h_var = small(TILES)
        h_rstd = small(TILES)
        h_shift = small(TILES)
        v_six = small(TILES, 6)
        v_mv = small(TILES, 2)
        v_var = small(TILES)
        v_rstd = small(TILES)
        v_neg_mean = small(TILES)
        v_shift = small(TILES)
        v_amax = small(G)
        w_amax = small(4)
        w_amax_all = small(4)
        w_safe = small(4)
        w_pow2 = small(4)
        w_inv = small(4)
        w_mul = small(4)
        dinv_mul = small(2)
        bias_mul = small(1)
        ffn_scale = small(8)
        raw = vT[:, G - 5:G, :, :].rearrange("p g a b -> p (g a b)")
        w1_raw = raw[:, 0:FT * D].rearrange("p (k d) -> p k d", k=FT)
        w2_raw = raw[:, 1024:2048].rearrange("p (k f) -> p k f", k=DT)
        w1T_raw = raw[:, 2048:3072].rearrange("p (k f) -> p k f", k=DT)
        w2T_raw = raw[:, 3072:4096].rearrange("p (k d) -> p k d", k=FT)
        w2g_raw = raw[:, 4096:5120].rearrange("p (k d) -> p k d", k=FT)
        more = vT[:, G - 6, :, :].rearrange("p a b -> p (a b)")
        ffn_raw = more[:, 0:512].rearrange("p (k d) -> p k d", k=DT)
        edge_rows = more[:, 512:1024]
        more2 = vT[:, 0:4, :, :].rearrange("p g a b -> p (g a b)")
        edge_cols = more2[:, 0:64].rearrange("p (k g) -> p k g", k=TILES)
        edge_rest = more2[:, 64:128].rearrange("p (k g) -> p k g", k=TILES)
        edge_rest2 = more2[:, 128:192].rearrange("p (k g) -> p k g", k=TILES)
        bias_f = more2[:, 256:512]
        bias_lo_f = more2[:, 512:640].bitcast(FP16)
        bias_hi_f = more2[:, 640:768].bitcast(FP16)
        wv = more2[:, 1024:1536]
        wc = more2[:, 1536:2048]
        wt = more2[:, 2048:2560]
        fv = [adj_in[:, 2 * p:2 * p + 2, :] for p in range(2)]
        fc = [H[p][:, :, :].rearrange("p a b -> p (a b)").bitcast(FP32).rearrange("p (a b) -> p a b", a=DT)
              for p in range(2)]
        fq = [HT[p][:, 0:DT, :].bitcast(BF16) for p in range(2)]

        bank = [ctx.enter_context(nc.psum_tensor(f"bank{i}", [PART, 512], FP32)) for i in range(8)]
        p_banks = [bank[0], bank[1], bank[2], bank[0]]
        p2_banks = [bank[1], bank[2], bank[0], bank[1]]
        o_banks = [bank[2], bank[0], bank[1], bank[2]]
        t_banks = [bank[3], bank[4], bank[5], bank[3]]
        z_banks = [bank[4], bank[5]]
        x_banks = [bank[3], bank[4]]
        a_banks = [bank[5], bank[3], bank[4], bank[5]]
        ht_banks = [bank[6], bank[7]]
        d_bank = bank[6]
        v_banks = [bank[7], bank[6]]

        y_banks = [[bank[0], bank[1]], [bank[2], bank[3]]]

        x_in, adj_fetched = sem("x_in"), sem("adj_fetched")
        w1_in, w2_in, ffn_in, edge_in, vec_in = sem("w1_in"), sem("w2_in"), sem("ffn_in"), sem("edge_in"), sem("vec_in")
        ident_zero, ident_done, consts_done, ident16_done = sem("ident_zero"), sem("ident_done"), sem("consts_done"), sem("ident16_done")
        edge_rows_zero, edge_rows_T, setup_vec = sem("edge_rows_zero"), sem("edge_rows_T"), sem("setup_vec")
        w1_T, w2_T, bias_T = sem("w1_T"), sem("w2_T"), sem("bias_T")
        w1T_copied, w2T_copied = sem("w1T_copied"), sem("w2T_copied")
        amax_rows, amax_all, scales_done = sem("amax_rows"), sem("amax_all"), sem("scales_done")
        w1_hi_done, w2_hi_done, weights_done, edge_w_done, bias_done = (
            sem("w1_hi_done"), sem("w2_hi_done"), sem("weights_done"), sem("edge_w_done"), sem("bias_done"))
        x_six_done, v_six_done, deg_steps, dinv_done, fc2_done = (
            sem("x_six_done"), sem("v_six_done"), sem("deg_steps"), sem("dinv_done"), sem("fc2_done"))
        x_moments, x_rstd_done, x_var_done, u_done, u_hi_done, u_lo_done, base_half, base_done = (
            sem("x_moments"), sem("x_rstd_done"), sem("x_var_done"), sem("u_done"), sem("u_hi_done"),
            sem("u_lo_done"), sem("base_half"), sem("base_done"))
        H_done, HT_psum, HT_done, edge_w_copied = sem("H_done"), sem("HT_psum"), sem("HT_done"), sem("edge_w_copied")
        p_psum, binv_done, m_hi_done, m_lo_done = sem("p_psum"), sem("binv_done"), sem("m_hi_done"), sem("m_lo_done")
        z_psum, z_hi_done, z_lo_done = sem("z_psum"), sem("z_hi_done"), sem("z_lo_done")
        d_psum, dve_chain = sem("d_psum"), sem("dve_chain")
        a_psum, a_done, relu_done, mean_done, sq_done = sem("a_psum"), sem("a_done"), sem("relu_done"), sem("mean_done"), sem("sq_done")
        h_var_done, h_rstd_done, h_shift_done, h_done = sem("h_var_done"), sem("h_rstd_done"), sem("h_shift_done"), sem("h_done")
        hT_psum, hT_hi_done, hT_lo_done = sem("hT_psum"), sem("hT_hi_done"), sem("hT_lo_done")
        xw_psum, xw_hi_done, xw_lo_done = sem("xw_psum"), sem("xw_hi_done"), sem("xw_lo_done")
        p2_psum, m2_hi_done, m2_lo_done = sem("p2_psum"), sem("m2_hi_done"), sem("m2_lo_done")
        o_psum, x1_done, v_moments = sem("o_psum"), sem("x1_done"), sem("v_moments")
        v_var_done, v_shift_done, v_rstd_done, v_done, v_amax_done = (
            sem("v_var_done"), sem("v_shift_done"), sem("v_rstd_done"), sem("v_done"), sem("v_amax_done"))
        vT_psum, vT_done = sem("vT_psum"), sem("vT_done")
        row_amax_done, all_amax_done, ffn_scales_done = sem("row_amax_done"), sem("all_amax_done"), sem("ffn_scales_done")
        fv_done, fc_done, ft_done, fq_done, y_psum, y_done, out_stored = (
            sem("fv_done"), sem("fc_done"), sem("ft_done"), sem("fq_done"), sem("y_psum"), sem("y_done"), sem("out_stored"))

        block = ctx.enter_context(nc.Block())

        def wait(eng, semaphore, count):
            if isinstance(count, int) and count <= 0:
                return
            eng.wait_ge(semaphore, count)

        def run_steps(eng, step):
            for n in range(3):
                step(n, n % 2, n)
            with eng.Fori(3, G - 2, 2) as n:
                step(n, 1, None)
                step(n + 1, 0, None)
            for n in range(G - 1, G + 2):
                step(n, n % 2, n)

        FIRST_ORDER = ((True, (0, 1, 2)), (False, (0, 1, 2)), (True, (3,)), (False, (3,)))

        def live(at, g_ahead):
            return at is None or 0 <= at + g_ahead < G

        @block.sync
        def _(sp):
            sp.dma_start(x1[:, 0, :, :], x_dram[0]).then_inc(x_in, 16)
            sp.dma_start(adj_in[:, :, :], adj_dram[0]).then_inc(adj_fetched, 16)
            sp.dma_start(w1_raw, W1.rearrange("(k p) d -> p k d", p=PART)).then_inc(w1_in, 16)
            sp.dma_start(w2_raw, W2.rearrange("(k p) f -> p k f", p=PART)).then_inc(w2_in, 16)
            sp.dma_start(ffn_raw, ffn_w.rearrange("(k p) d -> p k d", p=PART)).then_inc(ffn_in, 16)

            def fetch(g):
                wait(sp, H_done, g)
                sp.dma_start(x1[:, bass.ds(g, 1), :, :], x_dram[bass.ds(g, 1)].rearrange("g p k d -> p g k d")).then_inc(x_in, 16)
                sp.dma_start(adj_in[:, :, :], adj_dram[bass.ds(g, 1)].rearrange("g p k e -> p (g k) e")).then_inc(adj_fetched, 16)

            with sp.Fori(1, G) as g:
                fetch(g)

            with sp.Fori(0, G) as g:
                sp.wait_ge(y_done, (g + 1) * PAIRS)
                sp.dma_start(out_dram[bass.ds(g, 1)].rearrange("g p k d -> p g k d"), x1[:, bass.ds(g, 1), :, :]).then_inc(out_stored, 16)
            sp.wait_ge(out_stored, 16 * G)

        @block.gpsimd
        def _(pool):
            nc.gpsimd.memset(ident[:, :], 0.0).then_inc(ident_zero, 1)
            pool.wait_ge(ident_zero, 1)
            nc.gpsimd.affine_select(out=ident[:, :], in_=ident[:, :], compare_op=ALU.not_equal, fill=1.0, base=0,
                                    pattern=[[-1, PART]], channel_multiplier=1).then_inc(ident_done, 1)
            nc.gpsimd.memset(minus_half[:, :], -0.5).then_inc(consts_done, 1)
            nc.gpsimd.memset(eps_col[:, :], EPS).then_inc(consts_done, 1)
            nc.gpsimd.memset(one_by_f[:, :], 1.0 / F).then_inc(consts_done, 1)
            nc.gpsimd.memset(u_hi[:, :, D:U_STRIDE], 1.0).then_inc(consts_done, 1)
            nc.gpsimd.memset(bias_lhs[:, :], X_SCALE).then_inc(consts_done, 1)
            pool.wait_ge(consts_done, 5)

            def x_inverse_std(g):
                pool.wait_ge(x_moments, g + 1)
                nc.gpsimd.tensor_tensor(x_var[:, :], x_mv[:, :, 1], eps_col[:, :], ALU.add).then_inc(x_var_done, 1)
                pool.wait_ge(x_var_done, g + 1)
                nc.gpsimd.tensor_tensor(x_rstd[:, :], x_var[:, :], minus_half[:, :], ALU.pow).then_inc(x_rstd_done, 1)

            def u_low_and_base(g):
                pool.wait_ge(u_hi_done, g + 1)
                wait(pool, p_psum, TILES * g)
                nc.gpsimd.tensor_tensor(u_lo[:, :, :], u[:, :, :], u_hi[:, :, 0:D], ALU.subtract).then_inc(u_lo_done, 1)
                nc.gpsimd.tensor_tensor(u[:, :, :], u[:, :, :], b2_all[:, :].unsqueeze(1).to_broadcast([PART, TILES, D]), ALU.add).then_inc(base_half, 1)
                pool.wait_ge(base_half, g + 1)
                nc.gpsimd.tensor_tensor(pool_gate[:, :], eps_col[:, :], eps_col[:, :], ALU.add)
                base = x1[:, bass.ds(g, 1), :, :].rearrange("p g k d -> p (g k) d")
                nc.gpsimd.tensor_tensor(base, base, u[:, :, :], ALU.add).then_inc(base_done, 1)

            def fetch_edge_w(g):
                wait(pool, d_psum, g)
                nc.gpsimd.tensor_copy(edge_w_now[:, :, :], edge_w[:, :, bass.ds(g, 1), :].rearrange("p k g c -> p (k g) c")).then_inc(edge_w_copied, 1)

            def h_inverse_std(g):
                pool.wait_ge(sq_done, TILES * (g + 1))
                nc.gpsimd.tensor_tensor(h_var[:, :], h_sq[:, :], one_by_f[:, :], ALU.mult).then_inc(h_var_done, 1)
                pool.wait_ge(h_var_done, 2 * g + 1)
                nc.gpsimd.tensor_tensor(h_var[:, :], h_var[:, :], eps_col[:, :], ALU.add).then_inc(h_var_done, 1)
                pool.wait_ge(h_var_done, 2 * g + 2)
                nc.gpsimd.tensor_tensor(h_rstd[:, :], h_var[:, :], minus_half[:, :], ALU.pow).then_inc(h_rstd_done, 1)
                pool.wait_ge(h_rstd_done, g + 1)
                nc.gpsimd.tensor_tensor(h_shift[:, :], h_neg_mean[:, :], h_rstd[:, :], ALU.mult).then_inc(h_shift_done, 1)

            def v_inverse_std(g):
                pool.wait_ge(v_moments, g + 1)
                nc.gpsimd.tensor_tensor(v_var[:, :], v_mv[:, :, 1], eps_col[:, :], ALU.add).then_inc(v_var_done, 1)
                nc.gpsimd.tensor_scalar(v_neg_mean[:, :], v_mv[:, :, 0], -1.0, 0.0, ALU.mult, ALU.add).then_inc(v_var_done, 1)
                pool.wait_ge(v_var_done, 2 * (g + 1))
                nc.gpsimd.tensor_tensor(v_rstd[:, :], v_var[:, :], minus_half[:, :], ALU.pow).then_inc(v_rstd_done, 1)
                pool.wait_ge(v_rstd_done, g + 1)
                nc.gpsimd.tensor_tensor(v_shift[:, :], v_neg_mean[:, :], v_rstd[:, :], ALU.mult).then_inc(v_shift_done, 1)

            x_inverse_std(0)
            pool.wait_ge(vec_in, 64)
            u_low_and_base(0)
            pool.wait_ge(amax_rows, 4)
            nc.gpsimd.partition_all_reduce(w_amax_all[:, :], w_amax[:, :], PART, ALL_REDUCE_MAX).then_inc(amax_all, 1)
            pool.wait_ge(edge_w_done, 3)
            fetch_edge_w(0)

            def step(n, par, at):
                if live(at, 1):
                    x_inverse_std(n + 1)
                    u_low_and_base(n + 1)
                    fetch_edge_w(n + 1)
                if live(at, 0):
                    h_inverse_std(n)
                if live(at, -1):
                    v_inverse_std(n - 1)

            run_steps(pool, step)

            pool.wait_ge(row_amax_done, 1)
            nc.gpsimd.partition_all_reduce(ffn_scale[:, 1:2], ffn_scale[:, 0:1], PART, ALL_REDUCE_MAX).then_inc(all_amax_done, 1)

        @block.scalar
        def _(act):
            act.wait_ge(edge_rows_zero, 1)
            act.dma_start(edge_rows[0:G, :], edge_w_dram).then_inc(edge_in, 16)
            act.dma_start(b1_all[:, :], b1.partition_broadcast(PART)).then_inc(vec_in, 16)
            act.dma_start(b2_all[:, :], b2.partition_broadcast(PART)).then_inc(vec_in, 16)
            with nc.allow_non_contiguous_dma(reason="two short vectors, once"):
                act.dma_start(gamma_col[:, :], gamma.rearrange("(k p) -> p k", p=PART)).then_inc(vec_in, 16)
                act.dma_start(beta_col[:, :], beta.rearrange("(k p) -> p k", p=PART)).then_inc(vec_in, 16)

            def u_high(g):
                act.wait_ge(u_done, TILES * (g + 1))
                wait(act, p_psum, TILES * g)
                nc.scalar.activation(u_hi[:, :, 0:D], u[:, :, :], ACT.Copy).then_inc(u_hi_done, 1)

            u_high(0)
            act.wait_ge(scales_done, 1)
            act.wait_ge(w1T_copied, DT)
            for k in range(DT):
                nc.scalar.activation(w1_hi[:, k, :], w1T_raw[:, k, :], ACT.Copy, scale=w_mul[:, 0:1]).then_inc(w1_hi_done, 1)
            act.wait_ge(w2T_copied, 2 * PAIRS)
            nc.scalar.activation(w2_hi[:, :, :], w2g_raw, ACT.Copy, scale=w_mul[:, 1:2]).then_inc(w2_hi_done, 1)

            def step(n, par, at):
                for is_m, tiles in FIRST_ORDER:
                    for j in tiles:
                        if is_m and live(at, 0):
                            act.wait_ge(binv_done, TILES * n + j + 1)
                            nc.scalar.activation(m_hi[:, j, :], p_banks[j][:, 0:D], ACT.Copy, scale=binv64[:, j:j + 1]).then_inc(m_hi_done, 1)
                        if not is_m and live(at, -1):
                            act.wait_ge(hT_psum, TILES * (n - 1) + j + 1)
                            nc.scalar.activation(hT_hi[:, j, :], t_banks[j][:, :], ACT.Copy).then_inc(hT_hi_done, 1)
                if live(at, 0):
                    for k in range(DT):
                        act.wait_ge(z_psum, DT * n + k + 1)
                        nc.scalar.activation(z_hi[:, k, :], z_banks[k][:, :], ACT.Copy, scale=Z_DOWN).then_inc(z_hi_done, 1)
                if live(at, -2):
                    act.wait_ge(v_shift_done, n - 1)
                    for t in range(TILES):
                        nc.scalar.activation(v[:, t, :], x1[:, bass.ds(n - 2, 1), t, :].rearrange("p g d -> p (g d)"), ACT.Identity,
                                             bias=v_shift[:, t:t + 1], scale=v_rstd[:, t:t + 1]).then_inc(v_done, 1)
                if live(at, -1):
                    act.wait_ge(xw_psum, PAIRS * (n - 1) + 1)
                    nc.scalar.activation(xw_hi[:, 0:2, :].rearrange("p a d -> p (a d)"), x_banks[0][:, :], ACT.Copy, scale=X_DOWN).then_inc(xw_hi_done, 1)
                if live(at, 1):
                    u_high(n + 1)
                if live(at, -1):
                    act.wait_ge(xw_psum, PAIRS * (n - 1) + 2)
                    nc.scalar.activation(xw_hi[:, 2:4, :].rearrange("p a d -> p (a d)"), x_banks[1][:, :], ACT.Copy, scale=X_DOWN).then_inc(xw_hi_done, 1)
                if live(at, 0):
                    for t in range(TILES):
                        act.wait_ge(a_done, TILES * n + t + 1)
                        nc.scalar.activation(h[:, t, :], h[:, t, :], ACT.Relu, accum_out=h_sum[:, t:t + 1]).then_inc(relu_done, 1)
                    act.wait_ge(mean_done, n + 1)
                for is_m, t in ((True, 0), (False, 0), (True, 1), (False, 1), (True, 2), (True, 3), (False, 2), (False, 3)):
                    if is_m and live(at, -1):
                        act.wait_ge(p2_psum, TILES * (n - 1) + t + 1)
                        nc.scalar.activation(m_hi[:, t, :], p2_banks[t][:, 0:D], ACT.Copy, scale=binv[1 - par][:, t:t + 1]).then_inc(m2_hi_done, 1)
                    if not is_m and live(at, 0):
                        nc.scalar.activation(squares[t], h[:, t, :], ACT.Square, bias=h_neg_mean[:, t:t + 1],
                                             accum_out=h_sq[:, t:t + 1]).then_inc(sq_done, 1)
                if live(at, -2):
                    for k in range(DT):
                        act.wait_ge(vT_psum, DT * (n - 2) + k + 1)
                        nc.scalar.activation(vT[:, bass.ds(n - 2, 1), k, :].rearrange("p g c -> p (g c)"), v_banks[k][:, :], ACT.Copy).then_inc(vT_done, 1)
                if live(at, 0):
                    act.wait_ge(h_shift_done, n + 1)
                    for t in range(TILES):
                        nc.scalar.activation(h[:, t, :], h[:, t, :], ACT.Identity,
                                             bias=h_shift[:, t:t + 1], scale=h_rstd[:, t:t + 1]).then_inc(h_done, 1)

            run_steps(act, step)

            act.wait_ge(ffn_scales_done, 1)
            def scale_graph(g, par, first):
                if not first:
                    act.wait_ge(ft_done, g - 1)
                nc.scalar.activation(fv[par], vT[:, bass.ds(g, 1), :, :].rearrange("p g k c -> p (g k) c"), ACT.Abs,
                                     scale=ffn_scale[:, 4:5]).then_inc(fv_done, 1)

            scale_graph(0, 0, True)
            scale_graph(1, 1, True)
            with act.Fori(2, G - 1, 2) as g:
                scale_graph(g, 0, False)
                scale_graph(g + 1, 1, False)

        @block.vector
        def _(dve):
            chain = [0]

            def link(ins, k=1):
                chain[0] += k
                ins.then_inc(setup_vec, 1)
                dve.wait_ge(setup_vec, chain[0])

            nc.vector.memset(edge_rows, 0.0).then_inc(edge_rows_zero, 1)
            nc.vector.memset(edge_w[:, :, :, :], 0.0).then_inc(edge_rows_zero, 1)
            nc.vector.memset(bias_row[:, :, :], 0.0).then_inc(edge_rows_zero, 1)
            dve.wait_ge(ident_done, 1)
            nc.vector.tensor_copy(ident16[:, :], ident[:, :]).then_inc(ident16_done, 1)

            def x_statistics(g):
                dve.wait_ge(x_in, 16 * (g + 1))
                nc.vector.memset(dve_gate[:, 0:1], 0.0)
                for t in range(TILES):
                    nc.vector.bn_stats(x_six[:, t, :], x1[:, bass.ds(g, 1), t, :].rearrange("p g d -> p (g d)")).then_inc(x_six_done, 1)
                dve.wait_ge(x_six_done, TILES * (g + 1))
                nc.vector.memset(dve_gate[:, 1:2], 0.0)
                for t in range(TILES):
                    ins = nc.vector.bn_aggr(x_mv[:, t, :], x_six[:, t, :])
                ins.then_inc(x_moments, 1)

            def make_u(g):
                dve.wait_ge(x_rstd_done, g + 1)
                wait(dve, base_done, g)
                for t in range(TILES):
                    nc.vector.tensor_scalar(u[:, t, :], x1[:, bass.ds(g, 1), t, :].rearrange("p g d -> p (g d)"),
                                            x_mv[:, t, 0:1], x_rstd[:, t:t + 1], ALU.subtract, ALU.mult).then_inc(u_done, 1)

            def make_mask(g, par):
                dve.wait_ge(adj_fetched, 16 * (g + 1))
                nc.vector.tensor_scalar(H[par][:, :, :], adj_in[:, :, :], 0.0, None, ALU.not_equal).then_inc(H_done, 1)

            x_statistics(0)
            make_mask(0, 0)
            make_u(0)

            dve.wait_ge(edge_rows_T, 1)
            edge_psum = bank[7][:, :].rearrange("p (k c) -> p k c", k=TILES)[:, :, 0:G]
            link(nc.vector.tensor_copy(edge_cols, edge_psum))
            nc.vector.tensor_copy(edge_w[:, :, :, 0], edge_cols).then_inc(edge_w_done, 1)
            dve.wait_ge(edge_w_done, 1)
            link(nc.vector.tensor_tensor(edge_rest, edge_cols, edge_w[:, :, :, 0], ALU.subtract))
            nc.vector.tensor_copy(edge_w[:, :, :, 1], edge_rest).then_inc(edge_w_done, 1)
            dve.wait_ge(edge_w_done, 2)
            link(nc.vector.tensor_tensor(edge_rest2, edge_rest, edge_w[:, :, :, 1], ALU.subtract))
            nc.vector.tensor_copy(edge_w[:, :, :, 2], edge_rest2).then_inc(edge_w_done, 1)

            dve.wait_ge(vec_in, 64)
            for k in range(DT):
                dve.wait_ge(w1_T, k + 1)
                nc.vector.tensor_copy(w1T_raw[:, k, :], bank[3 + k][:, :]).then_inc(w1T_copied, 1)
            for q in range(PAIRS):
                dve.wait_ge(w2_T, q + 1)
                pair = [bank[5], bank[2]][q][:, :].rearrange("p (k d) -> p k d", k=2)
                nc.vector.tensor_copy(w2T_raw[:, 2 * q:2 * q + 2, :], pair).then_inc(w2T_copied, 1)
                for k in range(2):
                    ins = nc.vector.tensor_scalar(w2g_raw[:, 2 * q + k, :], pair[:, k, :], gamma_col[:, 2 * q + k:2 * q + k + 1], None, ALU.mult)
                ins.then_inc(w2T_copied, 1)
            nc.vector.tensor_reduce(w_amax[:, 0:1], w1_raw, AX.XY, ALU.max, apply_absolute_value=True).then_inc(amax_rows, 1)
            dve.wait_ge(w2T_copied, 2 * PAIRS)
            nc.vector.tensor_reduce(w_amax[:, 1:2], w2g_raw, AX.XY, ALU.max, apply_absolute_value=True).then_inc(amax_rows, 1)
            dve.wait_ge(ffn_in, 16)
            nc.vector.tensor_reduce(w_amax[:, 2:3], ffn_raw, AX.XY, ALU.max, apply_absolute_value=True).then_inc(amax_rows, 1)
            dve.wait_ge(bias_T, 1)
            link(nc.vector.tensor_copy(bias_f, bank[1][:, 0:D]))
            link(nc.vector.tensor_reduce(w_amax[:, 3:4], bias_f, AX.X, ALU.max, apply_absolute_value=True))
            nc.vector.tensor_scalar(w_amax[:, 3:4], w_amax[:, 3:4], 1.0 / F, None, ALU.mult).then_inc(amax_rows, 1)

            dve.wait_ge(amax_all, 1)
            link(nc.vector.tensor_scalar(w_safe[:, :], w_amax_all[:, :], 1e-30, None, ALU.max))
            link(nc.vector.tensor_tensor(w_safe[:, 1:2], w_safe[:, 1:2], w_safe[:, 3:4], ALU.max))
            link(nc.vector.tensor_scalar(w_pow2[:, :].bitcast(U32), w_safe[:, :].bitcast(U32), EXPONENT, None, ALU.bitwise_and))
            link(nc.vector.reciprocal(w_inv[:, :], w_pow2[:, :]))
            link(nc.vector.tensor_scalar(w_mul[:, :], w_inv[:, :], W_SCALE, None, ALU.mult))
            link(nc.vector.tensor_scalar(dinv_mul[:, 0:1], w_pow2[:, 0:1], 1.0 / (Z_SCALE * W_SCALE), None, ALU.mult))
            link(nc.vector.tensor_scalar(dinv_mul[:, 1:2], w_pow2[:, 1:2], 1.0 / X_SCALE, None, ALU.mult))
            nc.vector.tensor_scalar(bias_mul[:, :], w_inv[:, 1:2], X_SCALE, None, ALU.mult).then_inc(scales_done, 1)
            dve.wait_ge(scales_done, 1)

            for k in range(DT):
                dve.wait_ge(w1_hi_done, k + 1)
                nc.vector.scalar_tensor_tensor(w1_lo[:, k, :], w1T_raw[:, k, :], w_mul[:, 0:1], w1_hi[:, k, :],
                                               ALU.mult, ALU.subtract).then_inc(weights_done, 1)
            dve.wait_ge(w2_hi_done, 1)
            nc.vector.scalar_tensor_tensor(w2_lo[:, :, :], w2g_raw, w_mul[:, 1:2], w2_hi[:, :, :],
                                           ALU.mult, ALU.subtract).then_inc(weights_done, 1)
            link(nc.vector.tensor_scalar(bias_f, bias_f, bias_mul[:, :], None, ALU.mult))
            link(nc.vector.tensor_copy(bias_hi_f, bias_f))
            link(nc.vector.tensor_tensor(bias_lo_f, bias_f, bias_hi_f, ALU.subtract))
            for q in range(PAIRS):
                nc.vector.tensor_copy(bias_row[0:1, q, :], bias_hi_f[0:1, :]).then_inc(bias_done, 1)
                nc.vector.tensor_copy(bias_row[32:33, q, :], bias_lo_f[32:33, :]).then_inc(bias_done, 1)

            link(nc.vector.tensor_scalar(w_safe[:, 2:3], w_amax_all[:, 2:3], AMAX_FLOOR, None, ALU.max))
            link(nc.vector.reciprocal(w_inv[:, 2:3], w_safe[:, 2:3]))
            link(nc.vector.tensor_scalar(w_mul[:, 2:3], w_inv[:, 2:3], FP8_MAX, None, ALU.mult))
            link(nc.vector.reciprocal(ffn_scale[:, 6:7], w_mul[:, 2:3]))
            link(nc.vector.tensor_scalar(wv, ffn_raw.rearrange("p k d -> p (k d)"), w_mul[:, 2:3], None, ALU.mult))
            link(nc.vector.scalar_tensor_tensor(wc, wv, -1.0, wv, ALU.mult, ALU.max))
            link(nc.vector.tensor_scalar(wc, wc, ROUND_FLOOR, ROUND_SCALE, ALU.max, ALU.mult))
            link(nc.vector.tensor_tensor(wt, wv, wc, ALU.add))
            link(nc.vector.tensor_tensor(wq[:, :, :].rearrange("p k d -> p (k d)"), wt, wc, ALU.subtract))

            def step(n, par, at):
                if live(at, 0):
                    for j in range(2):
                        dve.wait_ge(HT_psum, 2 * n + j + 1)
                        nc.vector.tensor_copy(HT[par][:, 2 * j:2 * j + 2, :].rearrange("p a c -> p (a c)"),
                                              ht_banks[j][:, :].bitcast(FP16)).then_inc(HT_done, 1)

                def m_low(j):
                    dve.wait_ge(m_hi_done, TILES * n + j + 1)
                    nc.vector.scalar_tensor_tensor(m_lo[:, j, :], p_banks[j][:, 0:D], binv64[:, j:j + 1], m_hi[:, j, :],
                                                   ALU.mult, ALU.subtract).then_inc(m_lo_done, 1)

                def h_low(t):
                    dve.wait_ge(hT_hi_done, TILES * (n - 1) + t + 1)
                    nc.vector.tensor_tensor(hT_lo[:, t, :], t_banks[t][:, :], hT_hi[:, t, :], ALU.subtract).then_inc(hT_lo_done, 1)

                def invert_count(j):
                    dve.wait_ge(p_psum, TILES * n + j + 1)
                    nc.vector.tensor_scalar(count64[:, j:j + 1], p_banks[j][:, D:D + 1], 1.0, 1.0 / M_SCALE, ALU.max, ALU.mult).then_inc(dve_chain, 1)
                    dve.wait_ge(dve_chain, 5 * n + j + 1)
                    nc.vector.reciprocal(binv64[:, j:j + 1], count64[:, j:j + 1]).then_inc(binv_done, 1)

                for work, j in ((invert_count, 0), (invert_count, 1), (m_low, 0), (invert_count, 2), (m_low, 1), (m_low, 2),
                                (h_low, 0), (h_low, 1), (invert_count, 3), (h_low, 2), (m_low, 3), (h_low, 3)):
                    if live(at, -1 if work is h_low else 0):
                        work(j)
                if live(at, 0):
                    dve.wait_ge(binv_done, TILES * (n + 1))
                    nc.vector.tensor_scalar(binv[par][:, :], binv64[:, :], 1.0 / M_SCALE, None, ALU.mult).then_inc(dve_chain, 1)
                if live(at, -2):
                    nc.vector.bn_stats(v_six[:, TILES - 1, :], x1[:, bass.ds(n - 2, 1), TILES - 1, :].rearrange("p g d -> p (g d)")).then_inc(v_six_done, 1)
                    dve.wait_ge(v_six_done, TILES * (n - 1))
                    nc.vector.memset(dve_gate[:, 2:3], 0.0)
                    for t in range(TILES):
                        ins = nc.vector.bn_aggr(v_mv[:, t, :], v_six[:, t, :])
                    ins.then_inc(v_moments, 1)
                if live(at, 1):
                    x_statistics(n + 1)
                if live(at, 0):
                    for k in range(DT):
                        dve.wait_ge(z_hi_done, DT * n + k + 1)
                        nc.vector.scalar_tensor_tensor(z_lo[:, k, :], z_banks[k][:, :], Z_DOWN, z_hi[:, k, :],
                                                       ALU.mult, ALU.subtract).then_inc(z_lo_done, 1)
                if live(at, 1):
                    make_u(n + 1)
                if live(at, 0):
                    dve.wait_ge(d_psum, n + 1)
                    nc.vector.tensor_reduce(deg[:, :], d_bank[:, 0:TILES * W_PAD].rearrange("p (k c) -> p k c", c=W_PAD), AX.X, ALU.add).then_inc(deg_steps, 1)
                    dve.wait_ge(deg_steps, 4 * n + 1)
                    nc.vector.tensor_scalar(deg_pos[:, :], deg[:, :], 0.0, None, ALU.is_gt)
                    nc.vector.tensor_scalar(deg_safe[:, :], deg[:, :], SMALLEST, None, ALU.max).then_inc(deg_steps, 1)
                    dve.wait_ge(deg_steps, 4 * n + 2)
                    nc.vector.reciprocal(deg_inv[:, :], deg_safe[:, :]).then_inc(deg_steps, 1)
                    dve.wait_ge(deg_steps, 4 * n + 3)
                    nc.vector.tensor_tensor(dinv[:, :], deg_inv[:, :], deg_pos[:, :], ALU.mult).then_inc(deg_steps, 1)
                    dve.wait_ge(deg_steps, 4 * n + 4)
                    nc.vector.tensor_scalar(dinv1[:, :], dinv[:, :], dinv_mul[:, 0:1], None, ALU.mult).then_inc(dinv_done, 1)
                    nc.vector.tensor_scalar(dinv2[par][:, :], dinv[:, :], dinv_mul[:, 1:2], None, ALU.mult).then_inc(dinv_done, 1)
                for q in range(PAIRS):
                    if q == 1 and live(at, -2):
                        dve.wait_ge(v_done, TILES * (n - 1))
                        nc.vector.tensor_reduce(v_amax[:, bass.ds(n - 2, 1)], v[:, :, :], AX.XY, ALU.max, apply_absolute_value=True).then_inc(v_amax_done, 1)
                    if live(at, -1):
                        dve.wait_ge(xw_hi_done, PAIRS * (n - 1) + q + 1)
                        nc.vector.scalar_tensor_tensor(xw_lo[:, 2 * q:2 * q + 2, :].rearrange("p a d -> p (a d)"), x_banks[q][:, :], X_DOWN,
                                                       xw_hi[:, 2 * q:2 * q + 2, :].rearrange("p a d -> p (a d)"),
                                                       ALU.mult, ALU.subtract).then_inc(xw_lo_done, 1)
                if live(at, 0):
                    dve.wait_ge(dinv_done, 2 * (n + 1))
                    for t in range(TILES):
                        dve.wait_ge(a_psum, TILES * n + t + 1)
                        nc.vector.scalar_tensor_tensor(h[:, t, :], a_banks[t][:, :], dinv1[:, t:t + 1], b1_all[:, :],
                                                       ALU.mult, ALU.add).then_inc(a_done, 1)
                    dve.wait_ge(relu_done, TILES * (n + 1))
                    nc.vector.tensor_scalar(h_neg_mean[:, :], h_sum[:, :], -1.0 / F, None, ALU.mult).then_inc(mean_done, 1)
                if live(at, -1):
                    for t in range(TILES):
                        dve.wait_ge(m2_hi_done, TILES * (n - 1) + t + 1)
                        nc.vector.scalar_tensor_tensor(m_lo[:, t, :], p2_banks[t][:, 0:D], binv[1 - par][:, t:t + 1], m_hi[:, t, :],
                                                       ALU.mult, ALU.subtract).then_inc(m2_lo_done, 1)
                if live(at, 1):
                    make_mask(n + 1, 1 - par)
                if live(at, -1):
                    dve.wait_ge(base_done, n)
                    row = [x1[:, bass.ds(n - 1, 1), t, :].rearrange("p g d -> p (g d)") for t in range(TILES)]
                    for t in range(TILES):
                        if t >= 1:
                            dve.wait_ge(x1_done, TILES * (n - 1) + t)
                        dve.wait_ge(o_psum, TILES * (n - 1) + t + 1)
                        nc.vector.scalar_tensor_tensor(row[t], o_banks[t][:, 0:D], dinv2[1 - par][:, t:t + 1], row[t],
                                                       ALU.mult, ALU.add).then_inc(x1_done, 1)
                        if t >= 1:
                            nc.vector.bn_stats(v_six[:, t - 1, :], row[t - 1]).then_inc(v_six_done, 1)
                    dve.wait_ge(x1_done, TILES * n)
                    nc.vector.memset(dve_gate[:, 3:4], 0.0)

            run_steps(dve, step)

            dve.wait_ge(v_amax_done, G)
            nc.vector.tensor_reduce(ffn_scale[:, 0:1], v_amax[:, :], AX.X, ALU.max).then_inc(row_amax_done, 1)
            dve.wait_ge(all_amax_done, 1)
            link(nc.vector.tensor_scalar(ffn_scale[:, 2:3], ffn_scale[:, 1:2], AMAX_FLOOR, None, ALU.max))
            link(nc.vector.reciprocal(ffn_scale[:, 3:4], ffn_scale[:, 2:3]))
            link(nc.vector.tensor_scalar(ffn_scale[:, 4:5], ffn_scale[:, 3:4], FP8_MAX, None, ALU.mult))
            nc.vector.reciprocal(ffn_scale[:, 5:6], ffn_scale[:, 4:5]).then_inc(ffn_scales_done, 1)
            dve.wait_ge(ffn_scales_done, 1)
            link(nc.vector.tensor_tensor(ffn_scale[:, 7:8], ffn_scale[:, 5:6], ffn_scale[:, 6:7], ALU.mult))

            def round_graph(g, par, first):
                dve.wait_ge(fv_done, g + 1)
                nc.vector.tensor_scalar(fc[par], fv[par], ROUND_FLOOR, ROUND_SCALE, ALU.max, ALU.mult).then_inc(fc_done, 1)
                dve.wait_ge(fc_done, g + 1)
                nc.vector.scalar_tensor_tensor(fv[par], vT[:, bass.ds(g, 1), :, :].rearrange("p g k c -> p (g k) c"), ffn_scale[:, 4:5],
                                               fc[par], ALU.mult, ALU.add).then_inc(fc2_done, 1)
                dve.wait_ge(fc2_done, g + 1)
                if not first:
                    dve.wait_ge(y_psum, PAIRS * (g - 1))
                nc.vector.tensor_tensor(fq[par], fv[par], fc[par], ALU.subtract).then_inc(fq_done, 1)
                dve.wait_ge(fq_done, g + 1)
                dve.sem_inc(ft_done, 1)

            def finish_graph(g, par):
                for q in range(PAIRS):
                    dve.wait_ge(y_psum, PAIRS * g + q + 1)
                    row = x1[:, bass.ds(g, 1), 2 * q:2 * q + 2, :].rearrange("p g k d -> p (g k d)")
                    nc.vector.scalar_tensor_tensor(row, y_banks[par][q][:, :], ffn_scale[:, 7:8], row,
                                                   ALU.mult, ALU.add).then_inc(y_done, 1)

            round_graph(0, 0, True)
            round_graph(1, 1, True)
            finish_graph(0, 0)
            with dve.Fori(2, G - 1, 2) as g:
                round_graph(g, 0, False)
                finish_graph(g - 1, 1)
                round_graph(g + 1, 1, False)
                finish_graph(g, 0)
            finish_graph(G - 1, 1)

        @block.tensor
        def _(pe):
            pe.wait_ge(ident_done, 1)
            pe.wait_ge(edge_in, 16)
            for k in range(TILES):
                ins = nc.tensor.transpose(bank[7][:, PART * k:PART * (k + 1)], edge_rows[:, PART * k:PART * (k + 1)], ident[:, :])
            ins.then_inc(edge_rows_T, 1)
            pe.wait_ge(w1_in, 16)
            for k in range(DT):
                for f in range(FT):
                    ins = nc.tensor.transpose(bank[3 + k][:, PART * f:PART * (f + 1)], w1_raw[:, f, PART * k:PART * (k + 1)], ident[:, :])
                ins.then_inc(w1_T, 1)
            pe.wait_ge(w2_in, 16)
            for q in range(PAIRS):
                for kk in range(2):
                    for o in range(DT):
                        f = 2 * q + kk
                        ins = nc.tensor.transpose([bank[5], bank[2]][q][:, D * kk + PART * o:D * kk + PART * (o + 1)],
                                                  w2_raw[:, o, PART * f:PART * (f + 1)], ident[:, :])
                ins.then_inc(w2_T, 1)
            pe.wait_ge(vec_in, 64)
            pe.wait_ge(w2T_copied, 2 * PAIRS)
            for f in range(FT):
                ins = nc.tensor.matmul(bank[1][:, 0:D], beta_col[:, f:f + 1].to_broadcast([PART, PART]), w2T_raw[:, f, :],
                                       start=(f == 0), stop=(f == FT - 1))
            ins.then_inc(bias_T, 1)
            pe.wait_ge(ident16_done, 1)
            pe.wait_ge(consts_done, 5)

            def step(n, par, at):
                mask, maskT, old_mask, old_maskT = H[par], HT[par], H[1 - par], HT[1 - par]
                if live(at, 0):
                    pe.wait_ge(H_done, n + 1)
                    wait(pe, vT_done, DT * (n - 2))
                    wait(pe, dinv_done, 2 * n)
                    if at == 0:
                        pe.wait_ge(edge_w_done, 3)
                    for j in range(2):
                        for e in range(2):
                            for t in range(TILES):
                                ins = nc.tensor.transpose(
                                    ht_banks[j][:, :].bitcast(FP16)[:, C * e + PART * t:C * e + PART * (t + 1)],
                                    mask[:, t, PART * (2 * j + e):PART * (2 * j + e + 1)], ident16[:, :])
                        ins.then_inc(HT_psum, 1)
                    pe.wait_ge(u_lo_done, n + 1)
                    if at == 0:
                        pe.wait_ge(amax_rows, 4)

                def edge_sums(j):
                    if j < 3:
                        wait(pe, x1_done, TILES * (n - 2) + j + 2)
                    else:
                        pe.wait_ge(m_lo_done, TILES * n + 1)
                    for k in range(TILES):
                        nc.tensor.matmul(p_banks[j][:, 0:D + 1], mask[:, k, PART * j:PART * (j + 1)], u_hi[:, k, 0:D + 1],
                                         start=(k == 0), stop=False)
                        ins = nc.tensor.matmul(p_banks[j][:, 0:D], mask[:, k, PART * j:PART * (j + 1)], u_lo[:, k, :],
                                               start=False, stop=(k == TILES - 1))
                    ins.then_inc(p_psum, 1)

                def transpose_h(t):
                    pe.wait_ge(h_done, TILES * (n - 1) + t + 1)
                    if t == 3:
                        pe.wait_ge(hT_lo_done, TILES * (n - 1) + 1)
                    for k in range(FT):
                        ins = nc.tensor.transpose(t_banks[t][:, PART * k:PART * (k + 1)], h[:, t, PART * k:PART * (k + 1)], ident[:, :])
                    ins.then_inc(hT_psum, 1)

                for is_m, tiles in FIRST_ORDER:
                    for j in tiles:
                        if is_m and live(at, 0):
                            edge_sums(j)
                        if not is_m and live(at, -1):
                            transpose_h(j)
                if live(at, 0):
                    pe.wait_ge(HT_done, 2 * (n + 1))
                    if at == 0:
                        pe.wait_ge(w1T_copied, DT)
                        pe.wait_ge(w2T_copied, 2 * PAIRS)
                    for d in range(DT):
                        wait(pe, hT_lo_done, TILES * (n - 1) + 2 + d)
                        for k in range(TILES):
                            if d == 0:
                                pe.wait_ge(m_lo_done, TILES * n + k + 1)
                            nc.tensor.matmul(z_banks[d][:, :], m_hi[:, k, PART * d:PART * (d + 1)], maskT[:, k, :], start=(k == 0), stop=False)
                            ins = nc.tensor.matmul(z_banks[d][:, :], m_lo[:, k, PART * d:PART * (d + 1)], maskT[:, k, :],
                                                   start=False, stop=(k == TILES - 1))
                        ins.then_inc(z_psum, 1)
                    pe.wait_ge(edge_w_copied, n + 1)
                    for t in range(TILES):
                        for k in range(TILES):
                            ins = nc.tensor.matmul(d_bank[:, W_PAD * t:W_PAD * (t + 1)], maskT[:, k, PART * t:PART * (t + 1)],
                                                   edge_w_now[:, k, :], start=(k == 0), stop=(k == TILES - 1))
                    ins.then_inc(d_psum, 1)
                if live(at, -1):
                    if at == 1:
                        pe.wait_ge(bias_done, 2 * PAIRS)
                        pe.wait_ge(weights_done, DT + 1)
                    pe.wait_ge(hT_lo_done, TILES * n)
                    for q in range(PAIRS):
                        if q == 1 and live(at, 0):
                            pe.wait_ge(z_lo_done, DT * n + 1)
                        nc.tensor.matmul(x_banks[q][:, :], bias_lhs[:, :], bias_row[:, :, :].rearrange("p a d -> p (a d)"), start=True, stop=False)
                        for tt in range(2):
                            t = 2 * q + tt
                            for k in range(FT):
                                dst = x_banks[q][:, D * tt:D * (tt + 1)]
                                hi, lo = hT_hi[:, t, PART * k:PART * (k + 1)], hT_lo[:, t, PART * k:PART * (k + 1)]
                                nc.tensor.matmul(dst, hi, w2_hi[:, k, :], start=False, stop=False)
                                nc.tensor.matmul(dst, hi, w2_lo[:, k, :], start=False, stop=False)
                                ins = nc.tensor.matmul(dst, lo, w2_hi[:, k, :], start=False, stop=(tt == 1 and k == FT - 1))
                        ins.then_inc(xw_psum, 1)
                if live(at, 0):
                    if at == 0:
                        pe.wait_ge(weights_done, DT)
                    pe.wait_ge(z_lo_done, DT * (n + 1))
                    for t in range(TILES):
                        if t in (1, 2):
                            wait(pe, xw_lo_done, PAIRS * (n - 1) + t)
                        if t == 3:
                            pe.wait_ge(a_done, TILES * n + 1)
                        for k in range(DT):
                            hi, lo = z_hi[:, k, PART * t:PART * (t + 1)], z_lo[:, k, PART * t:PART * (t + 1)]
                            nc.tensor.matmul(a_banks[t][:, :], hi, w1_hi[:, k, :], start=(k == 0), stop=False)
                            nc.tensor.matmul(a_banks[t][:, :], hi, w1_lo[:, k, :], start=False, stop=False)
                            ins = nc.tensor.matmul(a_banks[t][:, :], lo, w1_hi[:, k, :], start=False, stop=(k == DT - 1))
                        ins.then_inc(a_psum, 1)
                if live(at, -1):
                    pe.wait_ge(xw_lo_done, PAIRS * n)
                    for j in range(TILES):
                        if j < 3:
                            if live(at, 0):
                                pe.wait_ge(m_lo_done, TILES * n + j + 2)
                            else:
                                pe.wait_ge(x1_done, TILES * (n - 1))
                        else:
                            pe.wait_ge(m2_lo_done, TILES * (n - 1) + 1)
                        for k in range(TILES):
                            nc.tensor.matmul(p2_banks[j][:, 0:D], old_mask[:, k, PART * j:PART * (j + 1)], xw_hi[:, k, :], start=(k == 0), stop=False)
                            ins = nc.tensor.matmul(p2_banks[j][:, 0:D], old_mask[:, k, PART * j:PART * (j + 1)], xw_lo[:, k, :],
                                                   start=False, stop=(k == TILES - 1))
                        ins.then_inc(p2_psum, 1)
                if live(at, -2):
                    pe.wait_ge(v_done, TILES * (n - 1))
                    for k in range(DT):
                        if k == 1 and live(at, 0):
                            pe.wait_ge(dinv_done, 2 * (n + 1))
                        if k == 0 and live(at, 0):
                            pe.wait_ge(HT_done, 2 * (n + 1))
                        if not live(at, 0):
                            pe.wait_ge(vT_done, DT * (n - 2))
                        for t in range(TILES):
                            ins = nc.tensor.transpose(v_banks[k][:, PART * t:PART * (t + 1)], v[:, t, PART * k:PART * (k + 1)], ident[:, :])
                        ins.then_inc(vT_psum, 1)
                if live(at, -1):
                    pe.wait_ge(m2_lo_done, TILES * (n - 1) + 2)
                    for t in range(TILES):
                        if t == 3:
                            pe.wait_ge(x1_done, TILES * (n - 1) + 1)
                        for k in range(TILES):
                            if t == 0 and k >= 1:
                                pe.wait_ge(m2_lo_done, TILES * (n - 1) + k + 1)
                            nc.tensor.matmul(o_banks[t][:, 0:D], old_maskT[:, k, PART * t:PART * (t + 1)], m_hi[:, k, :], start=(k == 0), stop=False)
                            ins = nc.tensor.matmul(o_banks[t][:, 0:D], old_maskT[:, k, PART * t:PART * (t + 1)], m_lo[:, k, :],
                                                   start=False, stop=(k == TILES - 1))
                        ins.then_inc(o_psum, 1)

            run_steps(pe, step)

            pe.wait_ge(vT_done, DT * G)

            def multiply_graph(g, par, first):
                pe.wait_ge(fq_done, g + 1)
                for q in range(PAIRS):
                    if not first:
                        pe.wait_ge(y_done, PAIRS * (g - 2) + q + 1)
                    for tt in range(2):
                        t = 2 * q + tt
                        for k in range(DT):
                            ins = nc.tensor.matmul(y_banks[par][q][:, D * tt:D * (tt + 1)], fq[par][:, k, PART * t:PART * (t + 1)], wq[:, k, :],
                                                   start=(k == 0), stop=(k == DT - 1))
                    ins.then_inc(y_psum, 1)

            multiply_graph(0, 0, True)
            multiply_graph(1, 1, True)
            with pe.Fori(2, G - 1, 2) as g:
                multiply_graph(g, 0, False)
                multiply_graph(g + 1, 1, False)


_INS = ["x", "adj", "L0_gnn_W1", "L0_gnn_b1", "L0_gnn_gamma", "L0_gnn_beta", "L0_gnn_W2", "L0_gnn_b2", "L0_ffn_weight"]


def kernel(**inputs):
    import numpy as _np
    import concourse.bacc as _bacc
    from concourse import mybir as _mybir
    from concourse.bass_utils import run_bass_kernel_spmd as _run

    nc = _bacc.Bacc("TRN2", target_bir_lowering=False, num_devices=1)
    arrays, args = {}, []
    for name in _INS:
        a = _np.ascontiguousarray(inputs[name])
        arrays[f"in_{name}_dram"] = a
        args.append(nc.dram_tensor(f"in_{name}_dram", a.shape, _mybir.dt.from_np(a.dtype), kind="ExternalInput").ap())
    shape = arrays["in_x_dram"].shape
    args.append(nc.dram_tensor("out_0_dram", shape, _mybir.dt.float32, kind="ExternalOutput").ap())
    adjacency_gnn_then_fp8_ffn(nc, *args)
    r = _run(nc, [arrays], core_ids=[0])
    return r.results[0]["out_0_dram"]
```

```python
import concourse.bass as bass
from concourse import mybir
from concourse.alu_op_type import AluOpType as ALU
from contextlib import ExitStack


def adjacency_gnn_then_fp8_ffn(nc, x, adj, W1, b1, gamma, beta, W2, b2, ffn_w, out):
    FP32, FP16, BF16, U32 = mybir.dt.float32, mybir.dt.float16, mybir.dt.bfloat16, mybir.dt.uint32
    ACT = mybir.ActivationFunctionType
    AX = mybir.AxisListType
    ALL_REDUCE_MAX = bass.bass_isa.ReduceOp.max

    PART = 128
    G, C, D = x.shape
    F = W1.shape[0]
    TILES = C // PART
    DT = D // PART
    FT = F // PART
    assert (TILES, DT, FT) == (4, 2, 4) and G % 2 == 0 and G >= 6 and W2.shape == (D, F) and ffn_w.shape == (D, D)
    PAIRS = TILES // 2
    EPS = 1e-5
    FP8_MAX = 448.0
    AMAX_FLOOR = 1e-12
    SMALLEST = 1.2e-38
    M_SCALE = 64.0
    Z_DOWN = 1.0 / 16.0
    Z_SCALE = M_SCALE * Z_DOWN
    W_SCALE = 256.0
    X_DOWN = 1.0 / 16.0
    X_SCALE = W_SCALE * X_DOWN
    EXPONENT = 0x7F800000
    ROUND_FLOOR = 1.5 * 2.0 ** -6
    ROUND_SCALE = float(2 ** 20 - 1)
    W_PAD = 4
    U_STRIDE = D + 2

    x_dram = x.rearrange("g (p k) d -> g p k d", k=TILES)
    adj_dram = adj.rearrange("g (p k) e -> g p k e", k=TILES)
    out_dram = out.rearrange("g (p k) d -> g p k d", k=TILES)
    edge_w_dram = adj[:, 0, :]

    with ExitStack() as ctx:
        def sb(name, shape, dt):
            return ctx.enter_context(nc.sbuf_tensor(name, shape, dt))

        rows = sb("rows", [PART, 240], FP32)
        taken = [0]

        def small(*shape):
            size = 1
            for s in shape:
                size *= s
            at, taken[0] = taken[0], taken[0] + size
            part = rows[:, at:at + size]
            return part if len(shape) == 1 else part.rearrange("p (a b) -> p a b", b=shape[1])

        def sem(name):
            return ctx.enter_context(nc.semaphore(name))

        x1 = sb("x1", [PART, G, TILES, D], FP32)
        v = sb("v", [PART, G, TILES, D], FP32)
        w1_hi = sb("w1_hi", [PART, DT, F], FP16)
        w1_lo = sb("w1_lo", [PART, DT, F], FP16)
        w2_hi = sb("w2_hi", [PART, FT, D], FP16)
        w2_lo = sb("w2_lo", [PART, FT, D], FP16)
        wq = sb("wq", [PART, DT, D], BF16)
        b1_all = sb("b1_all", [PART, F], FP32)
        b2_all = sb("b2_all", [PART, D], FP32)
        gamma_col = sb("gamma_col", [PART, FT], FP32)
        beta_col = sb("beta_col", [PART, FT], FP32)
        ident = sb("ident", [PART, PART], FP32)
        ident16 = sb("ident16", [PART, PART], FP16)
        ident_bf = sb("ident_bf", [PART, PART], BF16)
        bias_row = sb("bias_row", [PART, PAIRS, D], FP16)
        bias_lhs = sb("bias_lhs", [PART, PART], FP16)
        edge_w = sb("edge_w", [PART, TILES, G, W_PAD], BF16)
        edge_w_now = sb("edge_w_now", [PART, TILES, W_PAD], BF16)
        adj_in = sb("adj_in", [PART, TILES, C], FP32)
        H = [sb(f"H{p}", [PART, TILES, C], FP16) for p in range(2)]
        HT = [sb(f"HT{p}", [PART, TILES, C], FP16) for p in range(2)]
        u = sb("u", [PART, TILES, D], FP32)
        u_hi = sb("u_hi", [PART, TILES, U_STRIDE], FP16)
        u_lo = sb("u_lo", [PART, TILES, D], FP16)
        m_hi = sb("m_hi", [PART, TILES, D], FP16)
        m_lo = sb("m_lo", [PART, TILES, D], FP16)
        z_hi = sb("z_hi", [PART, DT, C], FP16)
        z_lo = sb("z_lo", [PART, DT, C], FP16)
        h = sb("h", [PART, TILES, F], FP32)
        squares = [part[:, k, :].bitcast(BF16) for part in (z_hi, z_lo) for k in range(DT)]
        hT_hi = sb("hT_hi", [PART, TILES, F], FP16)
        hT_lo = sb("hT_lo", [PART, TILES, F], FP16)
        xw_hi = sb("xw_hi", [PART, TILES, D], FP16)
        xw_lo = sb("xw_lo", [PART, TILES, D], FP16)
        minus_half = small(TILES)
        eps_col = small(TILES)
        one_by_f = small(TILES)
        pool_gate = small(TILES)
        dve_gate = small(4)
        x_six = small(TILES, 6)
        x_mv = small(TILES, 2)
        x_var = small(TILES)
        x_rstd = small(TILES)
        count64 = small(TILES)
        binv64 = small(TILES)
        binv = [small(TILES) for p in range(2)]
        deg = small(TILES)
        deg_pos = small(TILES)
        deg_safe = small(TILES)
        deg_inv = small(TILES)
        dinv = small(TILES)
        dinv1 = small(TILES)
        dinv2 = [small(TILES) for p in range(2)]
        h_sum = small(TILES)
        h_neg_mean = small(TILES)
        h_sq = small(TILES)
        h_var = small(TILES)
        h_rstd = small(TILES)
        h_shift = small(TILES)
        v_six = small(TILES, 6)
        v_mv = small(TILES, 2)
        v_var = small(TILES)
        v_rstd = small(TILES)
        v_neg_mean = small(TILES)
        v_shift = small(TILES)
        v_amax = small(G)
        w_amax = small(4)
        w_amax_all = small(4)
        w_safe = small(4)
        w_pow2 = small(4)
        w_inv = small(4)
        w_mul = small(4)
        dinv_mul = small(2)
        bias_mul = small(1)
        ffn_scale = small(8)
        setup = v[:, G - 8:G, :, :].rearrange("p g k d -> p (g k d)")
        w1_raw = setup[:, 0:1024].rearrange("p (k d) -> p k d", k=FT)
        w2_raw = setup[:, 1024:2048].rearrange("p (k f) -> p k f", k=DT)
        w1T_raw = setup[:, 2048:3072].rearrange("p (k f) -> p k f", k=DT)
        w2T_raw = setup[:, 3072:4096].rearrange("p (k d) -> p k d", k=FT)
        w2g_raw = setup[:, 4096:5120].rearrange("p (k d) -> p k d", k=FT)
        ffn_raw = setup[:, 5120:5632].rearrange("p (k d) -> p k d", k=DT)
        edge_rows = setup[:, 5632:6144]
        edge_cols = setup[:, 6144:6208].rearrange("p (k g) -> p k g", k=TILES)
        edge_rest = setup[:, 6208:6272].rearrange("p (k g) -> p k g", k=TILES)
        edge_rest2 = setup[:, 6272:6336].rearrange("p (k g) -> p k g", k=TILES)
        bias_f = setup[:, 6336:6592]
        bias_lo_f = setup[:, 6592:6720].bitcast(FP16)
        bias_hi_f = setup[:, 6720:6848].bitcast(FP16)
        wq_in = setup[:, 7168:7680]
        wq_rounder = setup[:, 7680:8192]
        wq_sum = setup[:, 0:512]
        q_abs = [h[:, 2 * p:2 * p + 2, :].rearrange("p a b -> p (a b)") for p in range(2)]
        q_sum = [adj_in[:, 2 * p:2 * p + 2, :].rearrange("p a b -> p (a b)") for p in range(2)]
        q_rounder = [H[p][:, :, :].rearrange("p a b -> p (a b)").bitcast(FP32) for p in range(2)]
        q_nat = [HT[p][:, 0:2, :].rearrange("p a b -> p (a b)").bitcast(BF16) for p in range(2)]
        qT = [HT[p][:, 2:4, :].bitcast(BF16) for p in range(2)]

        bank = [ctx.enter_context(nc.psum_tensor(f"bank{i}", [PART, 512], FP32)) for i in range(8)]
        p_banks = [bank[0], bank[1], bank[2], bank[0]]
        p2_banks = [bank[1], bank[2], bank[0], bank[1]]
        o_banks = [bank[2], bank[0], bank[1], bank[2]]
        t_banks = [bank[3], bank[4], bank[5], bank[3]]
        z_banks = [bank[4], bank[5]]
        x_banks = [bank[3], bank[4]]
        a_banks = [bank[5], bank[3], bank[4], bank[5]]
        ht_banks = [bank[6], bank[7]]
        d_bank = bank[6]
        y_banks = [[bank[0], bank[1]], [bank[2], bank[3]]]
        qT_banks = [bank[6], bank[7]]

        x_in, adj_fetched = sem("x_in"), sem("adj_fetched")
        w1_in, w2_in, ffn_in, edge_in, vec_in = sem("w1_in"), sem("w2_in"), sem("ffn_in"), sem("edge_in"), sem("vec_in")
        ident_zero, ident_done, consts_done, ident16_done = sem("ident_zero"), sem("ident_done"), sem("consts_done"), sem("ident16_done")
        edge_rows_zero, edge_rows_T, setup_vec = sem("edge_rows_zero"), sem("edge_rows_T"), sem("setup_vec")
        w1_T, w2_T, bias_T = sem("w1_T"), sem("w2_T"), sem("bias_T")
        w1T_copied, w2T_copied = sem("w1T_copied"), sem("w2T_copied")
        amax_rows, amax_all, scales_done = sem("amax_rows"), sem("amax_all"), sem("scales_done")
        w1_hi_done, w2_hi_done, weights_done, edge_w_done, bias_done = (
            sem("w1_hi_done"), sem("w2_hi_done"), sem("weights_done"), sem("edge_w_done"), sem("bias_done"))
        x_six_done, v_six_done, deg_steps, dinv_done, fc2_done = (
            sem("x_six_done"), sem("v_six_done"), sem("deg_steps"), sem("dinv_done"), sem("fc2_done"))
        x_moments, x_rstd_done, x_var_done, u_done, u_hi_done, u_lo_done, base_half, base_done = (
            sem("x_moments"), sem("x_rstd_done"), sem("x_var_done"), sem("u_done"), sem("u_hi_done"),
            sem("u_lo_done"), sem("base_half"), sem("base_done"))
        H_done, HT_psum, HT_done, edge_w_copied = sem("H_done"), sem("HT_psum"), sem("HT_done"), sem("edge_w_copied")
        p_psum, binv_done, m_hi_done, m_lo_done = sem("p_psum"), sem("binv_done"), sem("m_hi_done"), sem("m_lo_done")
        z_psum, z_hi_done, z_lo_done = sem("z_psum"), sem("z_hi_done"), sem("z_lo_done")
        d_psum, dve_chain = sem("d_psum"), sem("dve_chain")
        a_psum, a_done, relu_done, mean_done, sq_done = sem("a_psum"), sem("a_done"), sem("relu_done"), sem("mean_done"), sem("sq_done")
        h_var_done, h_rstd_done, h_shift_done = sem("h_var_done"), sem("h_rstd_done"), sem("h_shift_done")
        h_done, h_done_pool = sem("h_done"), sem("h_done_pool")
        hT_psum, hT_hi_done, hT_lo_done = sem("hT_psum"), sem("hT_hi_done"), sem("hT_lo_done")
        xw_psum, xw_hi_done, xw_lo_done = sem("xw_psum"), sem("xw_hi_done"), sem("xw_lo_done")
        p2_psum, m2_hi_done, m2_lo_done = sem("p2_psum"), sem("m2_hi_done"), sem("m2_lo_done")
        o_psum, x1_done, v_moments = sem("o_psum"), sem("x1_done"), sem("v_moments")
        v_var_done, v_shift_done, v_rstd_done, v_done, v_amax_done = (
            sem("v_var_done"), sem("v_shift_done"), sem("v_rstd_done"), sem("v_done"), sem("v_amax_done"))
        row_amax_done, all_amax_done, ffn_scales_done = sem("row_amax_done"), sem("all_amax_done"), sem("ffn_scales_done")
        q_abs_done, q_rounder_done, q_sum_done, q_done = sem("q_abs_done"), sem("q_rounder_done"), sem("q_sum_done"), sem("q_done")
        qT_psum, qT_done, y_psum, y_done, out_stored = sem("qT_psum"), sem("qT_done"), sem("y_psum"), sem("y_done"), sem("out_stored")

        block = ctx.enter_context(nc.Block())

        def wait(eng, semaphore, count):
            if isinstance(count, int) and count <= 0:
                return
            eng.wait_ge(semaphore, count)

        def run_steps(eng, step):
            for n in range(3):
                step(n, n % 2, n)
            with eng.Fori(3, G - 2, 2) as n:
                step(n, 1, None)
                step(n + 1, 0, None)
            for n in range(G - 1, G + 2):
                step(n, n % 2, n)

        def run_ffn_steps(eng, step):
            for n in range(2):
                step(n, n % 2, n)
            with eng.Fori(2, G - 3, 2) as n:
                step(n, 0, None)
                step(n + 1, 1, None)
            for n in range(G - 2, G + 2):
                step(n, n % 2, n)

        FIRST_ORDER = ((True, (0, 1, 2)), (False, (0, 1, 2)), (True, (3,)), (False, (3,)))

        def live(at, g_ahead):
            return at is None or 0 <= at + g_ahead < G

        @block.sync
        def _(sp):
            sp.dma_start(x1[:, 0, :, :], x_dram[0]).then_inc(x_in, 16)
            sp.dma_start(adj_in[:, :, :], adj_dram[0]).then_inc(adj_fetched, 16)
            sp.dma_start(w1_raw, W1.rearrange("(k p) d -> p k d", p=PART)).then_inc(w1_in, 16)
            sp.dma_start(w2_raw, W2.rearrange("(k p) f -> p k f", p=PART)).then_inc(w2_in, 16)
            sp.dma_start(ffn_raw, ffn_w.rearrange("(k p) d -> p k d", p=PART)).then_inc(ffn_in, 16)

            def fetch(g):
                wait(sp, H_done, g)
                sp.dma_start(x1[:, bass.ds(g, 1), :, :], x_dram[bass.ds(g, 1)].rearrange("g p k d -> p g k d")).then_inc(x_in, 16)
                sp.dma_start(adj_in[:, :, :], adj_dram[bass.ds(g, 1)].rearrange("g p k e -> p (g k) e")).then_inc(adj_fetched, 16)

            with sp.Fori(1, G) as g:
                fetch(g)

            with sp.Fori(0, G) as g:
                sp.wait_ge(y_done, (g + 1) * PAIRS)
                sp.dma_start(out_dram[bass.ds(g, 1)].rearrange("g p k d -> p g k d"), x1[:, bass.ds(g, 1), :, :]).then_inc(out_stored, 16)
            sp.wait_ge(out_stored, 16 * G)

        @block.gpsimd
        def _(pool):
            nc.gpsimd.memset(ident[:, :], 0.0).then_inc(ident_zero, 1)
            pool.wait_ge(ident_zero, 1)
            nc.gpsimd.affine_select(out=ident[:, :], in_=ident[:, :], compare_op=ALU.not_equal, fill=1.0, base=0,
                                    pattern=[[-1, PART]], channel_multiplier=1).then_inc(ident_done, 1)
            nc.gpsimd.memset(minus_half[:, :], -0.5).then_inc(consts_done, 1)
            nc.gpsimd.memset(eps_col[:, :], EPS).then_inc(consts_done, 1)
            nc.gpsimd.memset(one_by_f[:, :], 1.0 / F).then_inc(consts_done, 1)
            nc.gpsimd.memset(u_hi[:, :, D:U_STRIDE], 1.0).then_inc(consts_done, 1)
            nc.gpsimd.memset(bias_lhs[:, :], X_SCALE).then_inc(consts_done, 1)
            pool.wait_ge(consts_done, 5)

            def x_inverse_std(g):
                pool.wait_ge(x_moments, g + 1)
                nc.gpsimd.tensor_tensor(x_var[:, :], x_mv[:, :, 1], eps_col[:, :], ALU.add).then_inc(x_var_done, 1)
                pool.wait_ge(x_var_done, g + 1)
                nc.gpsimd.tensor_tensor(x_rstd[:, :], x_var[:, :], minus_half[:, :], ALU.pow).then_inc(x_rstd_done, 1)

            def u_low_and_base(g):
                pool.wait_ge(u_hi_done, g + 1)
                wait(pool, p_psum, TILES * g)
                nc.gpsimd.tensor_tensor(u_lo[:, :, :], u[:, :, :], u_hi[:, :, 0:D], ALU.subtract).then_inc(u_lo_done, 1)
                nc.gpsimd.tensor_tensor(u[:, :, :], u[:, :, :], b2_all[:, :].unsqueeze(1).to_broadcast([PART, TILES, D]), ALU.add).then_inc(base_half, 1)
                pool.wait_ge(base_half, g + 1)
                nc.gpsimd.tensor_tensor(pool_gate[:, :], eps_col[:, :], eps_col[:, :], ALU.add)
                base = x1[:, bass.ds(g, 1), :, :].rearrange("p g k d -> p (g k) d")
                nc.gpsimd.tensor_tensor(base, base, u[:, :, :], ALU.add).then_inc(base_done, 1)

            def fetch_edge_w(g):
                wait(pool, d_psum, g)
                nc.gpsimd.tensor_copy(edge_w_now[:, :, :], edge_w[:, :, bass.ds(g, 1), :].rearrange("p k g c -> p (k g) c")).then_inc(edge_w_copied, 1)

            def normalise_h(g):
                pool.wait_ge(sq_done, TILES * (g + 1))
                nc.gpsimd.tensor_tensor(h_var[:, :], h_sq[:, :], one_by_f[:, :], ALU.mult).then_inc(h_var_done, 1)
                pool.wait_ge(h_var_done, 2 * g + 1)
                nc.gpsimd.tensor_tensor(h_var[:, :], h_var[:, :], eps_col[:, :], ALU.add).then_inc(h_var_done, 1)
                pool.wait_ge(h_var_done, 2 * g + 2)
                nc.gpsimd.tensor_tensor(h_rstd[:, :], h_var[:, :], minus_half[:, :], ALU.pow).then_inc(h_rstd_done, 1)
                pool.wait_ge(h_rstd_done, g + 1)
                nc.gpsimd.tensor_tensor(h_shift[:, :], h_neg_mean[:, :], h_rstd[:, :], ALU.mult).then_inc(h_shift_done, 1)
                pool.wait_ge(h_shift_done, g + 1)
                nc.gpsimd.tensor_tensor(pool_gate[:, :], eps_col[:, :], eps_col[:, :], ALU.add)
                for t in (2, 3):
                    nc.gpsimd.tensor_scalar(h[:, t, :], h[:, t, :], h_rstd[:, t:t + 1], h_shift[:, t:t + 1], ALU.mult, ALU.add).then_inc(h_done_pool, 1)

            def v_inverse_std(g):
                pool.wait_ge(v_moments, g + 1)
                nc.gpsimd.tensor_tensor(v_var[:, :], v_mv[:, :, 1], eps_col[:, :], ALU.add).then_inc(v_var_done, 1)
                nc.gpsimd.tensor_scalar(v_neg_mean[:, :], v_mv[:, :, 0], -1.0, 0.0, ALU.mult, ALU.add).then_inc(v_var_done, 1)
                pool.wait_ge(v_var_done, 2 * (g + 1))
                nc.gpsimd.tensor_tensor(v_rstd[:, :], v_var[:, :], minus_half[:, :], ALU.pow).then_inc(v_rstd_done, 1)
                pool.wait_ge(v_rstd_done, g + 1)
                nc.gpsimd.tensor_tensor(v_shift[:, :], v_neg_mean[:, :], v_rstd[:, :], ALU.mult).then_inc(v_shift_done, 1)

            x_inverse_std(0)
            pool.wait_ge(vec_in, 64)
            u_low_and_base(0)
            pool.wait_ge(amax_rows, 4)
            nc.gpsimd.partition_all_reduce(w_amax_all[:, :], w_amax[:, :], PART, ALL_REDUCE_MAX).then_inc(amax_all, 1)
            pool.wait_ge(edge_w_done, 3)
            fetch_edge_w(0)

            def step(n, par, at):
                if live(at, 1):
                    x_inverse_std(n + 1)
                    u_low_and_base(n + 1)
                    fetch_edge_w(n + 1)
                if live(at, 0):
                    normalise_h(n)
                if live(at, -1):
                    v_inverse_std(n - 1)

            run_steps(pool, step)

            pool.wait_ge(row_amax_done, 1)
            nc.gpsimd.partition_all_reduce(ffn_scale[:, 1:2], ffn_scale[:, 0:1], PART, ALL_REDUCE_MAX).then_inc(all_amax_done, 1)

            def ffn_step(n, par, at):
                if live(at, 0):
                    pool.wait_ge(q_sum_done, n + 1)
                    wait(pool, qT_psum, n - 1)
                    nc.gpsimd.tensor_tensor(q_nat[par], q_sum[par], q_rounder[par], ALU.subtract).then_inc(q_done, 1)

            run_ffn_steps(pool, ffn_step)

        @block.scalar
        def _(act):
            act.wait_ge(edge_rows_zero, 1)
            act.dma_start(edge_rows[0:G, :], edge_w_dram).then_inc(edge_in, 16)
            act.dma_start(b1_all[:, :], b1.partition_broadcast(PART)).then_inc(vec_in, 16)
            act.dma_start(b2_all[:, :], b2.partition_broadcast(PART)).then_inc(vec_in, 16)
            with nc.allow_non_contiguous_dma(reason="two short vectors, once"):
                act.dma_start(gamma_col[:, :], gamma.rearrange("(k p) -> p k", p=PART)).then_inc(vec_in, 16)
                act.dma_start(beta_col[:, :], beta.rearrange("(k p) -> p k", p=PART)).then_inc(vec_in, 16)

            def u_high(g):
                act.wait_ge(u_done, TILES * (g + 1))
                wait(act, p_psum, TILES * g)
                nc.scalar.activation(u_hi[:, :, 0:D], u[:, :, :], ACT.Copy).then_inc(u_hi_done, 1)

            u_high(0)
            act.wait_ge(scales_done, 1)
            act.wait_ge(w1T_copied, DT)
            for k in range(DT):
                nc.scalar.activation(w1_hi[:, k, :], w1T_raw[:, k, :], ACT.Copy, scale=w_mul[:, 0:1]).then_inc(w1_hi_done, 1)
            act.wait_ge(w2T_copied, 2 * PAIRS)
            nc.scalar.activation(w2_hi[:, :, :], w2g_raw, ACT.Copy, scale=w_mul[:, 1:2]).then_inc(w2_hi_done, 1)

            def step(n, par, at):
                for is_m, tiles in FIRST_ORDER:
                    for j in tiles:
                        if is_m and live(at, 0):
                            act.wait_ge(binv_done, TILES * n + j + 1)
                            nc.scalar.activation(m_hi[:, j, :], p_banks[j][:, 0:D], ACT.Copy, scale=binv64[:, j:j + 1]).then_inc(m_hi_done, 1)
                        if not is_m and live(at, -1):
                            act.wait_ge(hT_psum, TILES * (n - 1) + j + 1)
                            nc.scalar.activation(hT_hi[:, j, :], t_banks[j][:, :], ACT.Copy).then_inc(hT_hi_done, 1)
                if live(at, 0):
                    for k in range(DT):
                        act.wait_ge(z_psum, DT * n + k + 1)
                        nc.scalar.activation(z_hi[:, k, :], z_banks[k][:, :], ACT.Copy, scale=Z_DOWN).then_inc(z_hi_done, 1)
                if live(at, -2):
                    act.wait_ge(v_shift_done, n - 1)
                    for t in range(TILES):
                        nc.scalar.activation(v[:, bass.ds(n - 2, 1), t, :].rearrange("p g d -> p (g d)"), x1[:, bass.ds(n - 2, 1), t, :].rearrange("p g d -> p (g d)"), ACT.Identity,
                                             bias=v_shift[:, t:t + 1], scale=v_rstd[:, t:t + 1]).then_inc(v_done, 1)
                if live(at, -1):
                    act.wait_ge(xw_psum, PAIRS * (n - 1) + 1)
                    nc.scalar.activation(xw_hi[:, 0:2, :].rearrange("p a d -> p (a d)"), x_banks[0][:, :], ACT.Copy, scale=X_DOWN).then_inc(xw_hi_done, 1)
                if live(at, 1):
                    u_high(n + 1)
                if live(at, -1):
                    act.wait_ge(xw_psum, PAIRS * (n - 1) + 2)
                    nc.scalar.activation(xw_hi[:, 2:4, :].rearrange("p a d -> p (a d)"), x_banks[1][:, :], ACT.Copy, scale=X_DOWN).then_inc(xw_hi_done, 1)
                if live(at, 0):
                    for t in range(TILES):
                        act.wait_ge(a_done, TILES * n + t + 1)
                        nc.scalar.activation(h[:, t, :], h[:, t, :], ACT.Relu, accum_out=h_sum[:, t:t + 1]).then_inc(relu_done, 1)
                for is_m, t in ((True, 0), (True, 1), (False, 0), (True, 2), (False, 1), (True, 3), (False, 2), (False, 3)):
                    if (is_m, t) == (False, 0) and live(at, 0):
                        act.wait_ge(mean_done, n + 1)
                    if is_m and live(at, -1):
                        act.wait_ge(p2_psum, TILES * (n - 1) + t + 1)
                        nc.scalar.activation(m_hi[:, t, :], p2_banks[t][:, 0:D], ACT.Copy, scale=binv[1 - par][:, t:t + 1]).then_inc(m2_hi_done, 1)
                    if not is_m and live(at, 0):
                        nc.scalar.activation(squares[t], h[:, t, :], ACT.Square, bias=h_neg_mean[:, t:t + 1],
                                             accum_out=h_sq[:, t:t + 1]).then_inc(sq_done, 1)
                if live(at, 0):
                    act.wait_ge(h_shift_done, n + 1)
                    for t in range(2):
                        nc.scalar.activation(h[:, t, :], h[:, t, :], ACT.Identity,
                                             bias=h_shift[:, t:t + 1], scale=h_rstd[:, t:t + 1]).then_inc(h_done, 1)

            run_steps(act, step)

            act.wait_ge(ffn_scales_done, 1)

            def magnitude(g, par, first):
                if not first:
                    act.wait_ge(q_rounder_done, g - 1)
                nc.scalar.activation(q_abs[par], v[:, bass.ds(g, 1), :, :].rearrange("p g k d -> p (g k d)"), ACT.Abs,
                                     scale=ffn_scale[:, 4:5]).then_inc(q_abs_done, 1)

            magnitude(0, 0, True)
            magnitude(1, 1, True)

            def ffn_step(n, par, at):
                if live(at, 2):
                    magnitude(n + 2, par, False)
                if live(at, 0):
                    act.wait_ge(qT_psum, n + 1)
                    wait(act, y_psum, PAIRS * (n - 1))
                    nc.scalar.activation(qT[par], qT_banks[par][:, :].bitcast(BF16).rearrange("p (k c) -> p k c", k=DT),
                                         ACT.Copy).then_inc(qT_done, 1)

            run_ffn_steps(act, ffn_step)

        @block.vector
        def _(dve):
            chain = [0]

            def link(ins, k=1):
                chain[0] += k
                ins.then_inc(setup_vec, 1)
                dve.wait_ge(setup_vec, chain[0])

            nc.vector.memset(edge_rows, 0.0).then_inc(edge_rows_zero, 1)
            nc.vector.memset(edge_w[:, :, :, :], 0.0).then_inc(edge_rows_zero, 1)
            nc.vector.memset(bias_row[:, :, :], 0.0).then_inc(edge_rows_zero, 1)
            dve.wait_ge(ident_done, 1)
            nc.vector.tensor_copy(ident16[:, :], ident[:, :]).then_inc(ident16_done, 1)
            nc.vector.tensor_copy(ident_bf[:, :], ident[:, :]).then_inc(ident16_done, 1)

            def x_statistics(g):
                dve.wait_ge(x_in, 16 * (g + 1))
                nc.vector.memset(dve_gate[:, 0:1], 0.0)
                for t in range(TILES):
                    nc.vector.bn_stats(x_six[:, t, :], x1[:, bass.ds(g, 1), t, :].rearrange("p g d -> p (g d)")).then_inc(x_six_done, 1)
                dve.wait_ge(x_six_done, TILES * (g + 1))
                nc.vector.memset(dve_gate[:, 1:2], 0.0)
                for t in range(TILES):
                    ins = nc.vector.bn_aggr(x_mv[:, t, :], x_six[:, t, :])
                ins.then_inc(x_moments, 1)

            def make_u(g):
                dve.wait_ge(x_rstd_done, g + 1)
                wait(dve, base_done, g)
                for t in range(TILES):
                    nc.vector.tensor_scalar(u[:, t, :], x1[:, bass.ds(g, 1), t, :].rearrange("p g d -> p (g d)"),
                                            x_mv[:, t, 0:1], x_rstd[:, t:t + 1], ALU.subtract, ALU.mult).then_inc(u_done, 1)

            def make_mask(g, par):
                dve.wait_ge(adj_fetched, 16 * (g + 1))
                nc.vector.tensor_scalar(H[par][:, :, :], adj_in[:, :, :], 0.0, None, ALU.not_equal).then_inc(H_done, 1)

            x_statistics(0)
            make_mask(0, 0)
            make_u(0)

            dve.wait_ge(edge_rows_T, 1)
            edge_psum = bank[7][:, :].rearrange("p (k c) -> p k c", k=TILES)[:, :, 0:G]
            link(nc.vector.tensor_copy(edge_cols, edge_psum))
            nc.vector.tensor_copy(edge_w[:, :, :, 0], edge_cols).then_inc(edge_w_done, 1)
            dve.wait_ge(edge_w_done, 1)
            link(nc.vector.tensor_tensor(edge_rest, edge_cols, edge_w[:, :, :, 0], ALU.subtract))
            nc.vector.tensor_copy(edge_w[:, :, :, 1], edge_rest).then_inc(edge_w_done, 1)
            dve.wait_ge(edge_w_done, 2)
            link(nc.vector.tensor_tensor(edge_rest2, edge_rest, edge_w[:, :, :, 1], ALU.subtract))
            nc.vector.tensor_copy(edge_w[:, :, :, 2], edge_rest2).then_inc(edge_w_done, 1)

            dve.wait_ge(vec_in, 64)
            for k in range(DT):
                dve.wait_ge(w1_T, k + 1)
                nc.vector.tensor_copy(w1T_raw[:, k, :], bank[3 + k][:, :]).then_inc(w1T_copied, 1)
            for q in range(PAIRS):
                dve.wait_ge(w2_T, q + 1)
                pair = [bank[5], bank[2]][q][:, :].rearrange("p (k d) -> p k d", k=2)
                nc.vector.tensor_copy(w2T_raw[:, 2 * q:2 * q + 2, :], pair).then_inc(w2T_copied, 1)
                for k in range(2):
                    ins = nc.vector.tensor_scalar(w2g_raw[:, 2 * q + k, :], pair[:, k, :], gamma_col[:, 2 * q + k:2 * q + k + 1], None, ALU.mult)
                ins.then_inc(w2T_copied, 1)
            nc.vector.tensor_reduce(w_amax[:, 0:1], w1_raw, AX.XY, ALU.max, apply_absolute_value=True).then_inc(amax_rows, 1)
            dve.wait_ge(w2T_copied, 2 * PAIRS)
            nc.vector.tensor_reduce(w_amax[:, 1:2], w2g_raw, AX.XY, ALU.max, apply_absolute_value=True).then_inc(amax_rows, 1)
            dve.wait_ge(ffn_in, 16)
            nc.vector.tensor_reduce(w_amax[:, 2:3], ffn_raw, AX.XY, ALU.max, apply_absolute_value=True).then_inc(amax_rows, 1)
            dve.wait_ge(bias_T, 1)
            link(nc.vector.tensor_copy(bias_f, bank[1][:, 0:D]))
            link(nc.vector.tensor_reduce(w_amax[:, 3:4], bias_f, AX.X, ALU.max, apply_absolute_value=True))
            nc.vector.tensor_scalar(w_amax[:, 3:4], w_amax[:, 3:4], 1.0 / F, None, ALU.mult).then_inc(amax_rows, 1)

            dve.wait_ge(amax_all, 1)
            link(nc.vector.tensor_scalar(w_safe[:, :], w_amax_all[:, :], 1e-30, None, ALU.max))
            link(nc.vector.tensor_tensor(w_safe[:, 1:2], w_safe[:, 1:2], w_safe[:, 3:4], ALU.max))
            link(nc.vector.tensor_scalar(w_pow2[:, :].bitcast(U32), w_safe[:, :].bitcast(U32), EXPONENT, None, ALU.bitwise_and))
            link(nc.vector.reciprocal(w_inv[:, :], w_pow2[:, :]))
            link(nc.vector.tensor_scalar(w_mul[:, :], w_inv[:, :], W_SCALE, None, ALU.mult))
            link(nc.vector.tensor_scalar(dinv_mul[:, 0:1], w_pow2[:, 0:1], 1.0 / (Z_SCALE * W_SCALE), None, ALU.mult))
            link(nc.vector.tensor_scalar(dinv_mul[:, 1:2], w_pow2[:, 1:2], 1.0 / X_SCALE, None, ALU.mult))
            nc.vector.tensor_scalar(bias_mul[:, :], w_inv[:, 1:2], X_SCALE, None, ALU.mult).then_inc(scales_done, 1)
            dve.wait_ge(scales_done, 1)

            for k in range(DT):
                dve.wait_ge(w1_hi_done, k + 1)
                nc.vector.scalar_tensor_tensor(w1_lo[:, k, :], w1T_raw[:, k, :], w_mul[:, 0:1], w1_hi[:, k, :],
                                               ALU.mult, ALU.subtract).then_inc(weights_done, 1)
            dve.wait_ge(w2_hi_done, 1)
            nc.vector.scalar_tensor_tensor(w2_lo[:, :, :], w2g_raw, w_mul[:, 1:2], w2_hi[:, :, :],
                                           ALU.mult, ALU.subtract).then_inc(weights_done, 1)
            link(nc.vector.tensor_scalar(bias_f, bias_f, bias_mul[:, :], None, ALU.mult))
            link(nc.vector.tensor_copy(bias_hi_f, bias_f))
            link(nc.vector.tensor_tensor(bias_lo_f, bias_f, bias_hi_f, ALU.subtract))
            for q in range(PAIRS):
                nc.vector.tensor_copy(bias_row[0:1, q, :], bias_hi_f[0:1, :]).then_inc(bias_done, 1)
                nc.vector.tensor_copy(bias_row[32:33, q, :], bias_lo_f[32:33, :]).then_inc(bias_done, 1)

            link(nc.vector.tensor_scalar(w_safe[:, 2:3], w_amax_all[:, 2:3], AMAX_FLOOR, None, ALU.max))
            link(nc.vector.reciprocal(w_inv[:, 2:3], w_safe[:, 2:3]))
            link(nc.vector.tensor_scalar(w_mul[:, 2:3], w_inv[:, 2:3], FP8_MAX, None, ALU.mult))
            link(nc.vector.reciprocal(ffn_scale[:, 6:7], w_mul[:, 2:3]))
            link(nc.vector.tensor_scalar(wq_in, ffn_raw.rearrange("p k d -> p (k d)"), w_mul[:, 2:3], None, ALU.mult))
            link(nc.vector.scalar_tensor_tensor(wq_rounder, wq_in, -1.0, wq_in, ALU.mult, ALU.max))
            link(nc.vector.tensor_scalar(wq_rounder, wq_rounder, ROUND_FLOOR, ROUND_SCALE, ALU.max, ALU.mult))
            link(nc.vector.tensor_tensor(wq_sum, wq_in, wq_rounder, ALU.add))
            link(nc.vector.tensor_tensor(wq[:, :, :].rearrange("p k d -> p (k d)"), wq_sum, wq_rounder, ALU.subtract))

            def step(n, par, at):
                def maskT_out(j):
                    dve.wait_ge(HT_psum, 2 * n + j + 1)
                    nc.vector.tensor_copy(HT[par][:, 2 * j:2 * j + 2, :].rearrange("p a c -> p (a c)"),
                                          ht_banks[j][:, :].bitcast(FP16)).then_inc(HT_done, 1)

                def m_low(j):
                    dve.wait_ge(m_hi_done, TILES * n + j + 1)
                    nc.vector.scalar_tensor_tensor(m_lo[:, j, :], p_banks[j][:, 0:D], binv64[:, j:j + 1], m_hi[:, j, :],
                                                   ALU.mult, ALU.subtract).then_inc(m_lo_done, 1)

                def h_low(t):
                    dve.wait_ge(hT_hi_done, TILES * (n - 1) + t + 1)
                    nc.vector.tensor_tensor(hT_lo[:, t, :], t_banks[t][:, :], hT_hi[:, t, :], ALU.subtract).then_inc(hT_lo_done, 1)

                def invert_count(j):
                    dve.wait_ge(p_psum, TILES * n + j + 1)
                    nc.vector.tensor_scalar(count64[:, j:j + 1], p_banks[j][:, D:D + 1], 1.0, 1.0 / M_SCALE, ALU.max, ALU.mult).then_inc(dve_chain, 1)
                    dve.wait_ge(dve_chain, 5 * n + j + 1)
                    nc.vector.reciprocal(binv64[:, j:j + 1], count64[:, j:j + 1]).then_inc(binv_done, 1)

                for work, j in ((maskT_out, 0), (invert_count, 0), (invert_count, 1), (m_low, 0), (invert_count, 2), (m_low, 1), (m_low, 2),
                                (h_low, 0), (h_low, 1), (invert_count, 3), (maskT_out, 1), (m_low, 3), (h_low, 2), (h_low, 3)):
                    if live(at, -1 if work is h_low else 0):
                        work(j)
                if live(at, 0):
                    dve.wait_ge(binv_done, TILES * (n + 1))
                    nc.vector.tensor_scalar(binv[par][:, :], binv64[:, :], 1.0 / M_SCALE, None, ALU.mult).then_inc(dve_chain, 1)
                if live(at, -2):
                    nc.vector.bn_stats(v_six[:, TILES - 1, :], x1[:, bass.ds(n - 2, 1), TILES - 1, :].rearrange("p g d -> p (g d)")).then_inc(v_six_done, 1)
                    dve.wait_ge(v_six_done, TILES * (n - 1))
                    nc.vector.memset(dve_gate[:, 2:3], 0.0)
                    for t in range(TILES):
                        ins = nc.vector.bn_aggr(v_mv[:, t, :], v_six[:, t, :])
                    ins.then_inc(v_moments, 1)
                if live(at, 1):
                    x_statistics(n + 1)
                if live(at, 0):
                    for k in range(DT):
                        dve.wait_ge(z_hi_done, DT * n + k + 1)
                        nc.vector.scalar_tensor_tensor(z_lo[:, k, :], z_banks[k][:, :], Z_DOWN, z_hi[:, k, :],
                                                       ALU.mult, ALU.subtract).then_inc(z_lo_done, 1)
                if live(at, 1):
                    make_u(n + 1)
                if live(at, 0):
                    dve.wait_ge(d_psum, n + 1)
                    nc.vector.tensor_reduce(deg[:, :], d_bank[:, 0:TILES * W_PAD].rearrange("p (k c) -> p k c", c=W_PAD), AX.X, ALU.add).then_inc(deg_steps, 1)
                    dve.wait_ge(deg_steps, 4 * n + 1)
                    nc.vector.tensor_scalar(deg_pos[:, :], deg[:, :], 0.0, None, ALU.is_gt)
                    nc.vector.tensor_scalar(deg_safe[:, :], deg[:, :], SMALLEST, None, ALU.max).then_inc(deg_steps, 1)
                    dve.wait_ge(deg_steps, 4 * n + 2)
                    nc.vector.reciprocal(deg_inv[:, :], deg_safe[:, :]).then_inc(deg_steps, 1)
                    dve.wait_ge(deg_steps, 4 * n + 3)
                    nc.vector.tensor_tensor(dinv[:, :], deg_inv[:, :], deg_pos[:, :], ALU.mult).then_inc(deg_steps, 1)
                    dve.wait_ge(deg_steps, 4 * n + 4)
                    nc.vector.tensor_scalar(dinv1[:, :], dinv[:, :], dinv_mul[:, 0:1], None, ALU.mult).then_inc(dinv_done, 1)
                    nc.vector.tensor_scalar(dinv2[par][:, :], dinv[:, :], dinv_mul[:, 1:2], None, ALU.mult).then_inc(dinv_done, 1)
                for q in range(PAIRS):
                    if q == 1 and live(at, -2):
                        dve.wait_ge(v_done, TILES * (n - 1))
                        nc.vector.tensor_reduce(v_amax[:, bass.ds(n - 2, 1)], v[:, bass.ds(n - 2, 1), :, :].rearrange("p g k d -> p (g k) d"), AX.XY, ALU.max, apply_absolute_value=True).then_inc(v_amax_done, 1)
                    if live(at, -1):
                        dve.wait_ge(xw_hi_done, PAIRS * (n - 1) + q + 1)
                        nc.vector.scalar_tensor_tensor(xw_lo[:, 2 * q:2 * q + 2, :].rearrange("p a d -> p (a d)"), x_banks[q][:, :], X_DOWN,
                                                       xw_hi[:, 2 * q:2 * q + 2, :].rearrange("p a d -> p (a d)"),
                                                       ALU.mult, ALU.subtract).then_inc(xw_lo_done, 1)
                if live(at, 0):
                    dve.wait_ge(dinv_done, 2 * (n + 1))
                    for t in range(TILES):
                        dve.wait_ge(a_psum, TILES * n + t + 1)
                        nc.vector.scalar_tensor_tensor(h[:, t, :], a_banks[t][:, :], dinv1[:, t:t + 1], b1_all[:, :],
                                                       ALU.mult, ALU.add).then_inc(a_done, 1)
                    dve.wait_ge(relu_done, TILES * (n + 1))
                    nc.vector.tensor_scalar(h_neg_mean[:, :], h_sum[:, :], -1.0 / F, None, ALU.mult).then_inc(mean_done, 1)
                if live(at, -1):
                    for t in range(TILES):
                        dve.wait_ge(m2_hi_done, TILES * (n - 1) + t + 1)
                        nc.vector.scalar_tensor_tensor(m_lo[:, t, :], p2_banks[t][:, 0:D], binv[1 - par][:, t:t + 1], m_hi[:, t, :],
                                                       ALU.mult, ALU.subtract).then_inc(m2_lo_done, 1)
                if live(at, 1):
                    make_mask(n + 1, 1 - par)
                if live(at, -1):
                    dve.wait_ge(base_done, n)
                    row = [x1[:, bass.ds(n - 1, 1), t, :].rearrange("p g d -> p (g d)") for t in range(TILES)]
                    for t in range(TILES):
                        if t >= 1:
                            dve.wait_ge(x1_done, TILES * (n - 1) + t)
                        dve.wait_ge(o_psum, TILES * (n - 1) + t + 1)
                        nc.vector.scalar_tensor_tensor(row[t], o_banks[t][:, 0:D], dinv2[1 - par][:, t:t + 1], row[t],
                                                       ALU.mult, ALU.add).then_inc(x1_done, 1)
                        if t >= 1:
                            nc.vector.bn_stats(v_six[:, t - 1, :], row[t - 1]).then_inc(v_six_done, 1)
                    dve.wait_ge(x1_done, TILES * n)
                    nc.vector.memset(dve_gate[:, 3:4], 0.0)

            run_steps(dve, step)

            dve.wait_ge(v_amax_done, G)
            nc.vector.tensor_reduce(ffn_scale[:, 0:1], v_amax[:, :], AX.X, ALU.max).then_inc(row_amax_done, 1)
            dve.wait_ge(all_amax_done, 1)
            link(nc.vector.tensor_scalar(ffn_scale[:, 2:3], ffn_scale[:, 1:2], AMAX_FLOOR, None, ALU.max))
            link(nc.vector.reciprocal(ffn_scale[:, 3:4], ffn_scale[:, 2:3]))
            link(nc.vector.tensor_scalar(ffn_scale[:, 4:5], ffn_scale[:, 3:4], FP8_MAX, None, ALU.mult))
            nc.vector.reciprocal(ffn_scale[:, 5:6], ffn_scale[:, 4:5]).then_inc(ffn_scales_done, 1)
            dve.wait_ge(ffn_scales_done, 1)
            link(nc.vector.tensor_tensor(ffn_scale[:, 7:8], ffn_scale[:, 5:6], ffn_scale[:, 6:7], ALU.mult))

            def rounder(g, par):
                dve.wait_ge(q_abs_done, g + 1)
                nc.vector.tensor_scalar(q_rounder[par], q_abs[par], ROUND_FLOOR, ROUND_SCALE, ALU.max, ALU.mult).then_inc(q_rounder_done, 1)

            rounder(0, 0)

            def ffn_step(n, par, at):
                if live(at, 0):
                    dve.wait_ge(q_rounder_done, n + 1)
                    nc.vector.scalar_tensor_tensor(q_sum[par], v[:, bass.ds(n, 1), :, :].rearrange("p g k d -> p (g k d)"), ffn_scale[:, 4:5],
                                                   q_rounder[par], ALU.mult, ALU.add).then_inc(q_sum_done, 1)
                if live(at, 1):
                    wait(dve, q_done, n)
                    rounder(n + 1, 1 - par)
                if live(at, -2):
                    for q in range(PAIRS):
                        dve.wait_ge(y_psum, PAIRS * (n - 2) + q + 1)
                        row = x1[:, bass.ds(n - 2, 1), 2 * q:2 * q + 2, :].rearrange("p g k d -> p (g k d)")
                        nc.vector.scalar_tensor_tensor(row, y_banks[par][q][:, :], ffn_scale[:, 7:8], row,
                                                       ALU.mult, ALU.add).then_inc(y_done, 1)

            run_ffn_steps(dve, ffn_step)

        @block.tensor
        def _(pe):
            pe.wait_ge(ident_done, 1)
            pe.wait_ge(edge_in, 16)
            for k in range(TILES):
                ins = nc.tensor.transpose(bank[7][:, PART * k:PART * (k + 1)], edge_rows[:, PART * k:PART * (k + 1)], ident[:, :])
            ins.then_inc(edge_rows_T, 1)
            pe.wait_ge(w1_in, 16)
            for k in range(DT):
                for f in range(FT):
                    ins = nc.tensor.transpose(bank[3 + k][:, PART * f:PART * (f + 1)], w1_raw[:, f, PART * k:PART * (k + 1)], ident[:, :])
                ins.then_inc(w1_T, 1)
            pe.wait_ge(w2_in, 16)
            for q in range(PAIRS):
                for kk in range(2):
                    for o in range(DT):
                        f = 2 * q + kk
                        ins = nc.tensor.transpose([bank[5], bank[2]][q][:, D * kk + PART * o:D * kk + PART * (o + 1)],
                                                  w2_raw[:, o, PART * f:PART * (f + 1)], ident[:, :])
                ins.then_inc(w2_T, 1)
            pe.wait_ge(vec_in, 64)
            pe.wait_ge(w2T_copied, 2 * PAIRS)
            for f in range(FT):
                ins = nc.tensor.matmul(bank[1][:, 0:D], beta_col[:, f:f + 1].to_broadcast([PART, PART]), w2T_raw[:, f, :],
                                       start=(f == 0), stop=(f == FT - 1))
            ins.then_inc(bias_T, 1)
            pe.wait_ge(ident16_done, 2)
            pe.wait_ge(consts_done, 5)

            def step(n, par, at):
                mask, maskT, old_mask, old_maskT = H[par], HT[par], H[1 - par], HT[1 - par]
                if live(at, 0):
                    pe.wait_ge(H_done, n + 1)
                    wait(pe, dinv_done, 2 * n)
                    if at == 0:
                        pe.wait_ge(edge_w_done, 3)
                    for j in range(2):
                        for e in range(2):
                            for t in range(TILES):
                                ins = nc.tensor.transpose(
                                    ht_banks[j][:, :].bitcast(FP16)[:, C * e + PART * t:C * e + PART * (t + 1)],
                                    mask[:, t, PART * (2 * j + e):PART * (2 * j + e + 1)], ident16[:, :])
                        ins.then_inc(HT_psum, 1)
                    pe.wait_ge(u_lo_done, n + 1)
                    if at == 0:
                        pe.wait_ge(amax_rows, 4)

                def edge_sums(j):
                    if j < 3:
                        wait(pe, x1_done, TILES * (n - 2) + j + 2)
                    else:
                        pe.wait_ge(m_lo_done, TILES * n + 1)
                    for k in range(TILES):
                        nc.tensor.matmul(p_banks[j][:, 0:D + 1], mask[:, k, PART * j:PART * (j + 1)], u_hi[:, k, 0:D + 1],
                                         start=(k == 0), stop=False)
                        ins = nc.tensor.matmul(p_banks[j][:, 0:D], mask[:, k, PART * j:PART * (j + 1)], u_lo[:, k, :],
                                               start=False, stop=(k == TILES - 1))
                    ins.then_inc(p_psum, 1)

                def transpose_h(t):
                    pe.wait_ge((h_done, h_done_pool)[t // 2], 2 * (n - 1) + t % 2 + 1)
                    if t == 3:
                        pe.wait_ge(hT_lo_done, TILES * (n - 1) + 1)
                    for k in range(FT):
                        ins = nc.tensor.transpose(t_banks[t][:, PART * k:PART * (k + 1)], h[:, t, PART * k:PART * (k + 1)], ident[:, :])
                    ins.then_inc(hT_psum, 1)

                for is_m, tiles in FIRST_ORDER:
                    for j in tiles:
                        if is_m and live(at, 0):
                            edge_sums(j)
                        if not is_m and live(at, -1):
                            transpose_h(j)
                if live(at, 0):
                    pe.wait_ge(HT_done, 2 * n + 1)
                    if at == 0:
                        pe.wait_ge(w1T_copied, DT)
                        pe.wait_ge(w2T_copied, 2 * PAIRS)
                    for d in range(DT):
                        wait(pe, hT_lo_done, TILES * (n - 1) + 2 + d)
                        for k in range(TILES):
                            if d == 0:
                                pe.wait_ge(m_lo_done, TILES * n + k + 1)
                                if k == 2:
                                    pe.wait_ge(HT_done, 2 * (n + 1))
                            nc.tensor.matmul(z_banks[d][:, :], m_hi[:, k, PART * d:PART * (d + 1)], maskT[:, k, :], start=(k == 0), stop=False)
                            ins = nc.tensor.matmul(z_banks[d][:, :], m_lo[:, k, PART * d:PART * (d + 1)], maskT[:, k, :],
                                                   start=False, stop=(k == TILES - 1))
                        ins.then_inc(z_psum, 1)
                    pe.wait_ge(edge_w_copied, n + 1)
                    for t in range(TILES):
                        for k in range(TILES):
                            ins = nc.tensor.matmul(d_bank[:, W_PAD * t:W_PAD * (t + 1)], maskT[:, k, PART * t:PART * (t + 1)],
                                                   edge_w_now[:, k, :], start=(k == 0), stop=(k == TILES - 1))
                    ins.then_inc(d_psum, 1)
                if live(at, -1):
                    if at == 1:
                        pe.wait_ge(bias_done, 2 * PAIRS)
                        pe.wait_ge(weights_done, DT + 1)
                    pe.wait_ge(hT_lo_done, TILES * n)
                    for q in range(PAIRS):
                        if q == 1 and live(at, 0):
                            pe.wait_ge(z_lo_done, DT * n + 1)
                        nc.tensor.matmul(x_banks[q][:, :], bias_lhs[:, :], bias_row[:, :, :].rearrange("p a d -> p (a d)"), start=True, stop=False)
                        for tt in range(2):
                            t = 2 * q + tt
                            for k in range(FT):
                                dst = x_banks[q][:, D * tt:D * (tt + 1)]
                                hi, lo = hT_hi[:, t, PART * k:PART * (k + 1)], hT_lo[:, t, PART * k:PART * (k + 1)]
                                nc.tensor.matmul(dst, hi, w2_hi[:, k, :], start=False, stop=False)
                                nc.tensor.matmul(dst, hi, w2_lo[:, k, :], start=False, stop=False)
                                ins = nc.tensor.matmul(dst, lo, w2_hi[:, k, :], start=False, stop=(tt == 1 and k == FT - 1))
                        ins.then_inc(xw_psum, 1)
                if live(at, 0):
                    if at == 0:
                        pe.wait_ge(weights_done, DT)
                    pe.wait_ge(z_lo_done, DT * (n + 1))
                    for t in range(TILES):
                        if t in (1, 2):
                            wait(pe, xw_lo_done, PAIRS * (n - 1) + t)
                        if t == 3:
                            pe.wait_ge(a_done, TILES * n + 1)
                        for k in range(DT):
                            hi, lo = z_hi[:, k, PART * t:PART * (t + 1)], z_lo[:, k, PART * t:PART * (t + 1)]
                            nc.tensor.matmul(a_banks[t][:, :], hi, w1_hi[:, k, :], start=(k == 0), stop=False)
                            nc.tensor.matmul(a_banks[t][:, :], hi, w1_lo[:, k, :], start=False, stop=False)
                            ins = nc.tensor.matmul(a_banks[t][:, :], lo, w1_hi[:, k, :], start=False, stop=(k == DT - 1))
                        ins.then_inc(a_psum, 1)
                if live(at, -1):
                    pe.wait_ge(xw_lo_done, PAIRS * n)
                    for j in range(TILES):
                        if j < 3:
                            if live(at, 0):
                                pe.wait_ge(m_lo_done, TILES * n + j + 2)
                            else:
                                pe.wait_ge(x1_done, TILES * (n - 1))
                        else:
                            pe.wait_ge(m2_lo_done, TILES * (n - 1) + 1)
                        for k in range(TILES):
                            nc.tensor.matmul(p2_banks[j][:, 0:D], old_mask[:, k, PART * j:PART * (j + 1)], xw_hi[:, k, :], start=(k == 0), stop=False)
                            ins = nc.tensor.matmul(p2_banks[j][:, 0:D], old_mask[:, k, PART * j:PART * (j + 1)], xw_lo[:, k, :],
                                                   start=False, stop=(k == TILES - 1))
                        ins.then_inc(p2_psum, 1)
                if live(at, -1):
                    for k in range(TILES):
                        pe.wait_ge(m2_lo_done, TILES * (n - 1) + max(k, 1) + 1)
                        for t in (range(1) if k < 2 else range(2)):
                            for kk in (range(3) if (t, k) == (1, 2) else (k,)):
                                nc.tensor.matmul(o_banks[t][:, 0:D], old_maskT[:, kk, PART * t:PART * (t + 1)], m_hi[:, kk, :], start=(kk == 0), stop=False)
                                ins = nc.tensor.matmul(o_banks[t][:, 0:D], old_maskT[:, kk, PART * t:PART * (t + 1)], m_lo[:, kk, :],
                                                       start=False, stop=(kk == TILES - 1))
                            if k == TILES - 1:
                                ins.then_inc(o_psum, 1)
                    for t in (2, 3):
                        if t == 3:
                            pe.wait_ge(x1_done, TILES * (n - 1) + 1)
                        for k in range(TILES):
                            nc.tensor.matmul(o_banks[t][:, 0:D], old_maskT[:, k, PART * t:PART * (t + 1)], m_hi[:, k, :], start=(k == 0), stop=False)
                            ins = nc.tensor.matmul(o_banks[t][:, 0:D], old_maskT[:, k, PART * t:PART * (t + 1)], m_lo[:, k, :],
                                                   start=False, stop=(k == TILES - 1))
                        ins.then_inc(o_psum, 1)

            run_steps(pe, step)

            def transpose_q(g, par):
                pe.wait_ge(q_done, g + 1)
                for k in range(DT):
                    for t in range(TILES):
                        ins = nc.tensor.transpose(qT_banks[par][:, :].bitcast(BF16)[:, C * k + PART * t:C * k + PART * (t + 1)],
                                                  q_nat[par][:, D * t + PART * k:D * t + PART * (k + 1)], ident_bf[:, :])
                ins.then_inc(qT_psum, 1)

            def ffn_step(n, par, at):
                if live(at, 0):
                    transpose_q(n, par)
                    pe.wait_ge(qT_done, n + 1)
                    for q in range(PAIRS):
                        wait(pe, y_done, PAIRS * (n - 2) + q + 1)
                        for tt in range(2):
                            t = 2 * q + tt
                            for k in range(DT):
                                ins = nc.tensor.matmul(y_banks[par][q][:, D * tt:D * (tt + 1)], qT[par][:, k, PART * t:PART * (t + 1)], wq[:, k, :],
                                                       start=(k == 0), stop=(k == DT - 1))
                        ins.then_inc(y_psum, 1)

            pe.wait_ge(x1_done, TILES * G)
            run_ffn_steps(pe, ffn_step)


_INS = ["x", "adj", "L0_gnn_W1", "L0_gnn_b1", "L0_gnn_gamma", "L0_gnn_beta", "L0_gnn_W2", "L0_gnn_b2", "L0_ffn_weight"]


def kernel(**inputs):
    import numpy as _np
    import concourse.bacc as _bacc
    from concourse import mybir as _mybir
    from concourse.bass_utils import run_bass_kernel_spmd as _run

    nc = _bacc.Bacc("TRN2", target_bir_lowering=False, num_devices=1)
    arrays, args = {}, []
    for name in _INS:
        a = _np.ascontiguousarray(inputs[name])
        arrays[f"in_{name}_dram"] = a
        args.append(nc.dram_tensor(f"in_{name}_dram", a.shape, _mybir.dt.from_np(a.dtype), kind="ExternalInput").ap())
    shape = arrays["in_x_dram"].shape
    args.append(nc.dram_tensor("out_0_dram", shape, _mybir.dt.float32, kind="ExternalOutput").ap())
    adjacency_gnn_then_fp8_ffn(nc, *args)
    r = _run(nc, [arrays], core_ids=[0])
    return r.results[0]["out_0_dram"]
```

```python
import concourse.bass as bass
from concourse import mybir
from concourse.alu_op_type import AluOpType as ALU
from contextlib import ExitStack


def adjacency_gnn_then_fp8_ffn(nc, x, adj, W1, b1, gamma, beta, W2, b2, ffn_w, out):
    FP32, FP16, BF16, U32 = mybir.dt.float32, mybir.dt.float16, mybir.dt.bfloat16, mybir.dt.uint32
    ACT = mybir.ActivationFunctionType
    AX = mybir.AxisListType
    ALL_REDUCE_MAX = bass.bass_isa.ReduceOp.max

    PART = 128
    G, C, D = x.shape
    F = W1.shape[0]
    TILES = C // PART
    DT = D // PART
    FT = F // PART
    assert (TILES, DT, FT) == (4, 2, 4) and G % 2 == 0 and G >= 8 and W2.shape == (D, F) and ffn_w.shape == (D, D)
    PAIRS = TILES // 2
    EPS = 1e-5
    FP8_MAX = 448.0
    AMAX_FLOOR = 1e-12
    SMALLEST = 1.2e-38
    M_SCALE = 64.0
    Z_DOWN = 1.0 / 16.0
    Z_SCALE = M_SCALE * Z_DOWN
    W_SCALE = 256.0
    X_DOWN = 1.0 / 16.0
    X_SCALE = W_SCALE * X_DOWN
    EXPONENT = 0x7F800000
    WEIGHT_FLOOR = 1e-30
    ROUND_FLOOR = 1.5 * 2.0 ** -6
    ROUND_SCALE = float(2 ** 20 - 1)
    W_PAD = 4
    U_STRIDE = D + 2

    x_dram = x.rearrange("g (p k) d -> g p k d", k=TILES)
    adj_dram = adj.rearrange("g (p k) e -> g p k e", k=TILES)
    out_dram = out.rearrange("g (p k) d -> g p k d", k=TILES)
    edge_w_dram = adj[:, 0, :]

    with ExitStack() as ctx:
        def sb(name, shape, dt):
            return ctx.enter_context(nc.sbuf_tensor(name, shape, dt))

        rows = sb("rows", [PART, 240], FP32)
        taken = [0]

        def small(*shape):
            size = 1
            for s in shape:
                size *= s
            at, taken[0] = taken[0], taken[0] + size
            part = rows[:, at:at + size]
            return part if len(shape) == 1 else part.rearrange("p (a b) -> p a b", b=shape[1])

        def sem(name):
            return ctx.enter_context(nc.semaphore(name))

        x1 = sb("x1", [PART, G, TILES, D], FP32)
        v = sb("v", [PART, G, TILES, D], FP32)
        w1_hi = sb("w1_hi", [PART, DT, F], FP16)
        w1_lo = sb("w1_lo", [PART, DT, F], FP16)
        w2_hi = sb("w2_hi", [PART, FT, D], FP16)
        w2_lo = sb("w2_lo", [PART, FT, D], FP16)
        wq = sb("wq", [PART, DT, D], BF16)
        ffn_raw = sb("ffn_raw", [PART, DT * D], FP32)[:, :]
        b1_all = sb("b1_all", [PART, F], FP32)
        b2_all = sb("b2_all", [PART, D], FP32)
        gamma_col = sb("gamma_col", [PART, FT], FP32)
        beta_col = sb("beta_col", [PART, FT], FP32)
        ident = sb("ident", [PART, PART], FP32)
        ident16 = sb("ident16", [PART, PART], FP16)
        ident_bf = sb("ident_bf", [PART, PART], BF16)
        beta_w2 = sb("beta_w2", [PART, D], FP32)
        edge_w = sb("edge_w", [PART, TILES, G, W_PAD], BF16)
        edge_w_now = sb("edge_w_now", [PART, TILES, W_PAD], BF16)
        adj_in = sb("adj_in", [PART, TILES, C], FP32)
        H = [sb(f"H{p}", [PART, TILES, C], FP16) for p in range(2)]
        HT = [sb(f"HT{p}", [PART, TILES, C], FP16) for p in range(2)]
        u = sb("u", [PART, TILES, D], FP32)
        u_hi = sb("u_hi", [PART, TILES, U_STRIDE], FP16)
        u_lo = sb("u_lo", [PART, TILES, D], FP16)
        m_hi = sb("m_hi", [PART, TILES, D], FP16)
        m_lo = sb("m_lo", [PART, TILES, D], FP16)
        z_hi = sb("z_hi", [PART, DT, C], FP16)
        z_lo = sb("z_lo", [PART, DT, C], FP16)
        h = sb("h", [PART, TILES, F], FP32)
        squares = [part[:, k, :].bitcast(BF16) for part in (z_hi, z_lo) for k in range(DT)]
        hT_hi = sb("hT_hi", [PART, TILES, F], FP16)
        hT_lo = sb("hT_lo", [PART, TILES, F], FP16)
        xw = [hT_hi[:, 2 * q:2 * q + 2, :].rearrange("p a b -> p (a b)").bitcast(FP32) for q in range(PAIRS)]
        xw_hi = sb("xw_hi", [PART, TILES, D], FP16)
        xw_lo = sb("xw_lo", [PART, TILES, D], FP16)
        minus_half = small(TILES)
        eps_col = small(TILES)
        one_by_f = small(TILES)
        pool_gate = small(TILES)
        dve_gate = small(4)
        x_six = small(TILES, 6)
        x_mv = small(TILES, 2)
        x_var = small(TILES)
        x_rstd = small(TILES)
        count64 = small(TILES)
        binv64 = small(TILES)
        binv = [small(TILES) for p in range(2)]
        deg = small(TILES)
        deg_pos = small(TILES)
        deg_safe = small(TILES)
        deg_inv = small(TILES)
        dinv = small(TILES)
        dinv1 = small(TILES)
        dinv2 = [small(TILES) for p in range(2)]
        h_sum = small(TILES)
        h_neg_mean = small(TILES)
        h_sq = small(TILES)
        h_var = small(TILES)
        h_rstd = small(TILES)
        h_shift = small(TILES)
        v_six = small(TILES, 6)
        v_mv = small(TILES, 2)
        v_var = small(TILES)
        v_rstd = small(TILES)
        v_neg_mean = small(TILES)
        v_shift = small(TILES)
        v_amax = small(G + 1)
        w_amax = small(4)
        w_amax_all = small(4)
        w_safe = small(4)
        w_pow2 = small(4)
        w_inv = small(4)
        w_mul = small(4)
        dinv_mul = small(2)
        bias_mul = small(1)
        bias_col = small(DT)
        ffn_scale = small(8)
        setup = v[:, G - 8:G, :, :].rearrange("p g k d -> p (g k d)")
        w1_raw = setup[:, 0:1024].rearrange("p (k d) -> p k d", k=FT)
        w2_raw = setup[:, 1024:2048].rearrange("p (k f) -> p k f", k=DT)
        w1T_raw = setup[:, 2048:3072].rearrange("p (k f) -> p k f", k=DT)
        w2T_raw = setup[:, 3072:4096].rearrange("p (k d) -> p k d", k=FT)
        w2g_raw = setup[:, 4096:5120].rearrange("p (k d) -> p k d", k=FT)
        edge_rows = setup[:, 5120:5632]
        edge_cols = setup[:, 5632:5696].rearrange("p (k g) -> p k g", k=TILES)
        edge_rest = setup[:, 5696:5760].rearrange("p (k g) -> p k g", k=TILES)
        edge_rest2 = setup[:, 5760:5824].rearrange("p (k g) -> p k g", k=TILES)
        wq_in, wq_rounder, wq_sum = adj_in[:, 0, :], adj_in[:, 1, :], adj_in[:, 2, :]
        q_abs = [h[:, 2 * p:2 * p + 2, :].rearrange("p a b -> p (a b)") for p in range(2)]
        q_sum = [adj_in[:, 2 * p:2 * p + 2, :].rearrange("p a b -> p (a b)") for p in range(2)]
        q_rounder = [H[p][:, :, :].rearrange("p a b -> p (a b)").bitcast(FP32) for p in range(2)]
        q_nat = [HT[p][:, 0:2, :].rearrange("p a b -> p (a b)").bitcast(BF16) for p in range(2)]
        qT = [HT[p][:, 2:4, :].bitcast(BF16) for p in range(2)]

        bank = [ctx.enter_context(nc.psum_tensor(f"bank{i}", [PART, 512], FP32)) for i in range(8)]
        def p_bank(j, at):
            return bank[7] if (j, at) == (3, 1) else bank[j % 3]

        def p2_bank(j, at):
            return bank[4] if (j, at) == (3, G) else bank[(j + 1) % 3]

        o_banks = [bank[5], bank[0], bank[1], bank[2]]

        def t_bank(t, at):
            return bank[0] if (t, at) == (3, 1) else bank[3 + t]

        z_banks = [bank[3], bank[4]]
        x_banks = [bank[5], bank[3]]
        a_banks = [bank[4], bank[5], bank[3], bank[4]]
        ht_banks = [bank[6], bank[7]]
        d_bank = bank[6]
        y_banks = [[bank[0], bank[1]], [bank[2], bank[3]]]
        qT_banks = [bank[6], bank[7]]

        x_in, adj_fetched = sem("x_in"), sem("adj_fetched")
        w1_in, w2_in, ffn_in, edge_in, vec_in = sem("w1_in"), sem("w2_in"), sem("ffn_in"), sem("edge_in"), sem("vec_in")
        ident_zero, ident_done, consts_done, ident16_done = sem("ident_zero"), sem("ident_done"), sem("consts_done"), sem("ident16_done")
        edge_rows_zero, edge_rows_T, setup_vec = sem("edge_rows_zero"), sem("edge_rows_T"), sem("setup_vec")
        w1_T, w2_T, bias_T = sem("w1_T"), sem("w2_T"), sem("bias_T")
        w1T_copied, w2T_copied = sem("w1T_copied"), sem("w2T_copied")
        amax_rows, amax_all, scales_done = sem("amax_rows"), sem("amax_all"), sem("scales_done")
        w2g_done, bias_col_psum, bias_col_done, bias_out = sem("w2g_done"), sem("bias_col_psum"), sem("bias_col_done"), sem("bias_out")
        w1_hi_done, w2_hi_done, weights_done, edge_w_done = (
            sem("w1_hi_done"), sem("w2_hi_done"), sem("weights_done"), sem("edge_w_done"))
        x_six_done, v_six_done, deg_steps, dinv1_done, dinv2_done = (
            sem("x_six_done"), sem("v_six_done"), sem("deg_steps"), sem("dinv1_done"), sem("dinv2_done"))
        x_moments, x_rstd_done, x_var_done, u_done, u_hi_done, u_lo_done, base_half, base_done = (
            sem("x_moments"), sem("x_rstd_done"), sem("x_var_done"), sem("u_done"), sem("u_hi_done"),
            sem("u_lo_done"), sem("base_half"), sem("base_done"))
        H_done, HT_psum, HT_done, edge_w_copied = sem("H_done"), sem("HT_psum"), sem("HT_done"), sem("edge_w_copied")
        p_psum, binv_done, m_hi_done, m_lo_done = sem("p_psum"), sem("binv_done"), sem("m_hi_done"), sem("m_lo_done")
        z_psum, z_hi_done, z_lo_done = sem("z_psum"), sem("z_hi_done"), sem("z_lo_done")
        d_psum, dve_chain = sem("d_psum"), sem("dve_chain")
        a_psum, a_done, relu_done, mean_done, sq_done = sem("a_psum"), sem("a_done"), sem("relu_done"), sem("mean_done"), sem("sq_done")
        h_var_done, h_rstd_done, h_shift_done = sem("h_var_done"), sem("h_rstd_done"), sem("h_shift_done")
        h_done, h_done_pool = sem("h_done"), sem("h_done_pool")
        hT_psum, hT_hi_done, hT_lo_done = sem("hT_psum"), sem("hT_hi_done"), sem("hT_lo_done")
        xw_done = sem("xw_done")
        xw_psum, xw_hi_done, xw_lo_done = sem("xw_psum"), sem("xw_hi_done"), sem("xw_lo_done")
        p2_psum, m2_hi_done, m2_lo_done = sem("p2_psum"), sem("m2_hi_done"), sem("m2_lo_done")
        o_psum, x1_done, v_moments = sem("o_psum"), sem("x1_done"), sem("v_moments")
        v_var_done, v_shift_done, v_rstd_done, v_done, v_amax_done = (
            sem("v_var_done"), sem("v_shift_done"), sem("v_rstd_done"), sem("v_done"), sem("v_amax_done"))
        row_amax_done, all_amax_done, ffn_scales_done = sem("row_amax_done"), sem("all_amax_done"), sem("ffn_scales_done")
        q_abs_done, q_rounder_done, q_sum_done, q_done = sem("q_abs_done"), sem("q_rounder_done"), sem("q_sum_done"), sem("q_done")
        q_ends_done = sem("q_ends_done")
        qT_psum, qT_done, y_psum, y_done, out_stored = sem("qT_psum"), sem("qT_done"), sem("y_psum"), sem("y_done"), sem("out_stored")

        block = ctx.enter_context(nc.Block())

        def wait(eng, semaphore, count):
            if isinstance(count, int) and count <= 0:
                return
            eng.wait_ge(semaphore, count)

        def run_steps(eng, step):
            for n in range(3):
                step(n, n % 2, n)
            with eng.Fori(3, G - 2, 2) as n:
                step(n, 1, None)
                step(n + 1, 0, None)
            for n in range(G - 1, G + 2):
                step(n, n % 2, n)

        def run_ffn_steps(eng, step):
            for n in range(4):
                step(n, n % 2, n)
            with eng.Fori(4, G - 5, 2) as n:
                step(n, 0, None)
                step(n + 1, 1, None)
            for n in range(G - 4, G + 2):
                step(n, n % 2, n)

        Q_ENDS = (0, 1, G - 1)

        def wait_q(eng, g, at, half=PAIRS - 1):
            if at in Q_ENDS:
                eng.wait_ge(q_ends_done, PAIRS * Q_ENDS.index(at) + half + 1)
            else:
                eng.wait_ge(q_done, PAIRS * (g - 2) + half + 1)

        def first_order(at):
            if at == 1:
                return ((True, (0, 1, 2, 3)), (False, (0, 1, 2, 3)))
            return ((True, (0, 1, 2)), (False, (0, 1, 2)), (True, (3,)), (False, (3,)))

        def live(at, g_ahead):
            return at is None or 0 <= at + g_ahead < G

        @block.sync
        def _(sp):
            def fetch_x(g):
                wait(sp, x_in, 16 * g)
                sp.dma_start(x1[:, bass.ds(g, 1), :, :], x_dram[bass.ds(g, 1)].rearrange("g p k d -> p g k d")).then_inc(x_in, 16)

            def fetch_adj(g):
                wait(sp, H_done, g)
                sp.dma_start(adj_in[:, :, :], adj_dram[bass.ds(g, 1)].rearrange("g p k e -> p (g k) e")).then_inc(adj_fetched, 16)

            fetch_x(0)
            fetch_adj(0)
            sp.dma_start(w1_raw, W1.rearrange("(k p) d -> p k d", p=PART)).then_inc(w1_in, 16)
            fetch_x(1)
            sp.dma_start(w2_raw, W2.rearrange("(k p) f -> p k f", p=PART)).then_inc(w2_in, 16)
            sp.dma_start(ffn_raw.rearrange("p (k d) -> p k d", k=DT), ffn_w.rearrange("(k p) d -> p k d", p=PART)).then_inc(ffn_in, 16)
            with sp.Fori(1, G - 1) as g:
                fetch_adj(g)
                fetch_x(g + 1)
            fetch_adj(G - 1)

            with sp.Fori(0, G) as g:
                sp.wait_ge(y_done, (g + 1) * PAIRS)
                sp.dma_start(out_dram[bass.ds(g, 1)].rearrange("g p k d -> p g k d"), x1[:, bass.ds(g, 1), :, :]).then_inc(out_stored, 16)
            sp.wait_ge(out_stored, 16 * G)

        @block.gpsimd
        def _(pool):
            nc.gpsimd.memset(ident[:, :], 0.0).then_inc(ident_zero, 1)
            pool.wait_ge(ident_zero, 1)
            nc.gpsimd.affine_select(out=ident[:, :], in_=ident[:, :], compare_op=ALU.not_equal, fill=1.0, base=0,
                                    pattern=[[-1, PART]], channel_multiplier=1).then_inc(ident_done, 1)
            nc.gpsimd.memset(minus_half[:, :], -0.5).then_inc(consts_done, 1)
            nc.gpsimd.memset(eps_col[:, :], EPS).then_inc(consts_done, 1)
            nc.gpsimd.memset(one_by_f[:, :], 1.0 / F).then_inc(consts_done, 1)
            nc.gpsimd.memset(u_hi[:, :, D:U_STRIDE], 1.0).then_inc(consts_done, 1)
            pool.wait_ge(consts_done, 4)

            def x_inverse_std(g):
                pool.wait_ge(x_moments, g + 1)
                nc.gpsimd.tensor_tensor(x_var[:, :], x_mv[:, :, 1], eps_col[:, :], ALU.add).then_inc(x_var_done, 1)
                pool.wait_ge(x_var_done, g + 1)
                nc.gpsimd.tensor_tensor(x_rstd[:, :], x_var[:, :], minus_half[:, :], ALU.pow).then_inc(x_rstd_done, 1)

            def u_low(g):
                pool.wait_ge(u_hi_done, g + 1)
                wait(pool, p_psum, TILES * g)
                nc.gpsimd.tensor_tensor(u_lo[:, :, :], u[:, :, :], u_hi[:, :, 0:D], ALU.subtract).then_inc(u_lo_done, 1)

            def make_base(g):
                nc.gpsimd.tensor_tensor(u[:, :, :], u[:, :, :], b2_all[:, :].unsqueeze(1).to_broadcast([PART, TILES, D]), ALU.add).then_inc(base_half, 1)
                pool.wait_ge(base_half, g + 1)
                nc.gpsimd.tensor_tensor(pool_gate[:, :], eps_col[:, :], eps_col[:, :], ALU.add)
                base = x1[:, bass.ds(g, 1), :, :].rearrange("p g k d -> p (g k) d")
                nc.gpsimd.tensor_tensor(base, base, u[:, :, :], ALU.add).then_inc(base_done, 1)

            def xw_low(g, q):
                pool.wait_ge(xw_hi_done, PAIRS * g + q + 1)
                nc.gpsimd.tensor_tensor(xw_lo[:, 2 * q:2 * q + 2, :].rearrange("p a d -> p (a d)"), xw[q],
                                        xw_hi[:, 2 * q:2 * q + 2, :].rearrange("p a d -> p (a d)"), ALU.subtract).then_inc(xw_lo_done, 1)

            def fetch_edge_w(g):
                wait(pool, d_psum, g)
                nc.gpsimd.tensor_copy(edge_w_now[:, :, :], edge_w[:, :, bass.ds(g, 1), :].rearrange("p k g c -> p (k g) c")).then_inc(edge_w_copied, 1)

            def normalise_h(g):
                pool.wait_ge(sq_done, TILES * (g + 1))
                nc.gpsimd.tensor_tensor(h_var[:, :], h_sq[:, :], one_by_f[:, :], ALU.mult).then_inc(h_var_done, 1)
                pool.wait_ge(h_var_done, 2 * g + 1)
                nc.gpsimd.tensor_tensor(h_var[:, :], h_var[:, :], eps_col[:, :], ALU.add).then_inc(h_var_done, 1)
                pool.wait_ge(h_var_done, 2 * g + 2)
                nc.gpsimd.tensor_tensor(h_rstd[:, :], h_var[:, :], minus_half[:, :], ALU.pow).then_inc(h_rstd_done, 1)
                pool.wait_ge(h_rstd_done, g + 1)
                nc.gpsimd.tensor_tensor(h_shift[:, :], h_neg_mean[:, :], h_rstd[:, :], ALU.mult).then_inc(h_shift_done, 1)
                pool.wait_ge(h_shift_done, g + 1)
                nc.gpsimd.tensor_tensor(pool_gate[:, :], eps_col[:, :], eps_col[:, :], ALU.add)
                for t in (2, 3):
                    nc.gpsimd.tensor_scalar(h[:, t, :], h[:, t, :], h_rstd[:, t:t + 1], h_shift[:, t:t + 1], ALU.mult, ALU.add).then_inc(h_done_pool, 1)

            def v_inverse_std(g):
                pool.wait_ge(v_moments, g + 1)
                nc.gpsimd.tensor_tensor(v_var[:, :], v_mv[:, :, 1], eps_col[:, :], ALU.add).then_inc(v_var_done, 1)
                nc.gpsimd.tensor_scalar(v_neg_mean[:, :], v_mv[:, :, 0], -1.0, 0.0, ALU.mult, ALU.add).then_inc(v_var_done, 1)
                pool.wait_ge(v_var_done, 2 * (g + 1))
                nc.gpsimd.tensor_tensor(v_rstd[:, :], v_var[:, :], minus_half[:, :], ALU.pow).then_inc(v_rstd_done, 1)
                pool.wait_ge(v_rstd_done, g + 1)
                nc.gpsimd.tensor_tensor(v_shift[:, :], v_neg_mean[:, :], v_rstd[:, :], ALU.mult).then_inc(v_shift_done, 1)

            x_inverse_std(0)
            u_low(0)
            pool.wait_ge(amax_rows, 1)
            nc.gpsimd.partition_all_reduce(w_amax_all[:, 0:1], w_amax[:, 0:1], PART, ALL_REDUCE_MAX).then_inc(amax_all, 1)
            pool.wait_ge(edge_w_done, 3)
            fetch_edge_w(0)
            pool.wait_ge(vec_in, 64)
            make_base(0)
            pool.wait_ge(w2T_copied, PAIRS)
            nc.gpsimd.tensor_tensor(w2g_raw, w2T_raw, gamma_col[:, :].unsqueeze(2).to_broadcast([PART, FT, D]),
                                    ALU.mult).then_inc(w2g_done, 1)

            def step(n, par, at):
                if live(at, 1):
                    x_inverse_std(n + 1)
                if live(at, -1):
                    xw_low(n - 1, 0)
                if live(at, 1):
                    u_low(n + 1)
                if live(at, -1):
                    xw_low(n - 1, 1)
                if live(at, 1):
                    if at != 0:
                        make_base(n + 1)
                    fetch_edge_w(n + 1)
                if at == 0:
                    pool.wait_ge(amax_rows, 4)
                    nc.gpsimd.partition_all_reduce(w_amax_all[:, 1:4], w_amax[:, 1:4], PART, ALL_REDUCE_MAX).then_inc(amax_all, 1)
                if live(at, 0):
                    normalise_h(n)
                if at == 0:
                    make_base(1)
                if live(at, -1):
                    v_inverse_std(n - 1)

            run_steps(pool, step)

            pool.wait_ge(row_amax_done, 1)
            nc.gpsimd.partition_all_reduce(ffn_scale[:, 1:2], ffn_scale[:, 0:1], PART, ALL_REDUCE_MAX).then_inc(all_amax_done, 1)

            def ffn_step(n, par, at):
                if live(at, 0) and at not in Q_ENDS:
                    pool.wait_ge(q_sum_done, n + 1)
                    wait(pool, qT_psum, PAIRS * (n - 1))
                    for half in range(PAIRS):
                        part = slice(2 * D * half, 2 * D * (half + 1))
                        nc.gpsimd.tensor_tensor(q_nat[par][:, part], q_sum[par][:, part], q_rounder[par][:, part], ALU.subtract).then_inc(q_done, 1)

            run_ffn_steps(pool, ffn_step)

        @block.scalar
        def _(act):
            act.wait_ge(edge_rows_zero, 1)
            act.dma_start(edge_rows[0:G, :], edge_w_dram).then_inc(edge_in, 16)
            act.dma_start(b1_all[:, :], b1.partition_broadcast(PART)).then_inc(vec_in, 16)
            act.dma_start(b2_all[:, :], b2.partition_broadcast(PART)).then_inc(vec_in, 16)
            with nc.allow_non_contiguous_dma(reason="two short vectors, once"):
                act.dma_start(gamma_col[:, :], gamma.rearrange("(k p) -> p k", p=PART)).then_inc(vec_in, 16)
                act.dma_start(beta_col[:, :], beta.rearrange("(k p) -> p k", p=PART)).then_inc(vec_in, 16)

            def u_high(g):
                act.wait_ge(u_done, TILES * (g + 1))
                wait(act, p_psum, TILES * g)
                nc.scalar.activation(u_hi[:, :, 0:D], u[:, :, :], ACT.Copy).then_inc(u_hi_done, 1)

            u_high(0)
            for k in range(DT):
                act.wait_ge(w1_T, k + 1)
                nc.scalar.activation(w1T_raw[:, k, :], bank[3 + k][:, :], ACT.Copy).then_inc(w1T_copied, 1)

            def step(n, par, at):
                for is_m, tiles in first_order(at):
                    for j in tiles:
                        if at == 0 and j == 3 and is_m:
                            act.wait_ge(scales_done, 1)
                            for k in range(DT):
                                nc.scalar.activation(w1_hi[:, k, :], w1T_raw[:, k, :], ACT.Copy, scale=w_mul[:, 0:1]).then_inc(w1_hi_done, 1)
                        if is_m and live(at, 0):
                            act.wait_ge(binv_done, TILES * n + j + 1)
                            nc.scalar.activation(m_hi[:, j, :], p_bank(j, at)[:, 0:D], ACT.Copy, scale=binv64[:, j:j + 1]).then_inc(m_hi_done, 1)
                        if not is_m and live(at, -1):
                            act.wait_ge(hT_psum, TILES * (n - 1) + j + 1)
                            nc.scalar.activation(hT_hi[:, j, :], t_bank(j, at)[:, :], ACT.Copy).then_inc(hT_hi_done, 1)
                if live(at, 0):
                    for k in range(DT):
                        act.wait_ge(z_psum, DT * n + k + 1)
                        nc.scalar.activation(z_hi[:, k, :], z_banks[k][:, :], ACT.Copy, scale=Z_DOWN).then_inc(z_hi_done, 1)
                if at == 0:
                    for q in range(PAIRS):
                        act.wait_ge(w2_T, q + 1)
                        nc.scalar.activation(w2T_raw[:, 2 * q:2 * q + 2, :].rearrange("p k d -> p (k d)"), bank[1 + q][:, :], ACT.Copy).then_inc(w2T_copied, 1)

                def normalise_v():
                    act.wait_ge(v_shift_done, n - 1)
                    for t in range(TILES):
                        nc.scalar.activation(v[:, bass.ds(n - 2, 1), t, :].rearrange("p g d -> p (g d)"), x1[:, bass.ds(n - 2, 1), t, :].rearrange("p g d -> p (g d)"), ACT.Identity,
                                             bias=v_shift[:, t:t + 1], scale=v_rstd[:, t:t + 1]).then_inc(v_done, 1)

                if live(at, -2) and at != G:
                    normalise_v()
                if live(at, -1):
                    act.wait_ge(xw_done, PAIRS * (n - 1) + 1)
                    nc.scalar.activation(xw_hi[:, 0:2, :].rearrange("p a d -> p (a d)"), xw[0], ACT.Copy).then_inc(xw_hi_done, 1)
                if live(at, 1) and at != 0:
                    u_high(n + 1)
                if live(at, -1):
                    act.wait_ge(xw_done, PAIRS * (n - 1) + 2)
                    nc.scalar.activation(xw_hi[:, 2:4, :].rearrange("p a d -> p (a d)"), xw[1], ACT.Copy).then_inc(xw_hi_done, 1)
                if at == G:
                    normalise_v()
                if live(at, 0):
                    for t in range(TILES):
                        if at == 0 and t == 2:
                            u_high(1)
                        act.wait_ge(a_done, TILES * n + t + 1)
                        nc.scalar.activation(h[:, t, :], h[:, t, :], ACT.Relu, accum_out=h_sum[:, t:t + 1]).then_inc(relu_done, 1)
                for is_m, t in ((True, 0), (True, 1), (False, 0), (True, 2), (False, 1), (True, 3), (False, 2), (False, 3)):
                    if (is_m, t) == (False, 0) and live(at, 0):
                        act.wait_ge(mean_done, n + 1)
                    if is_m and live(at, -1):
                        act.wait_ge(p2_psum, TILES * (n - 1) + t + 1)
                        nc.scalar.activation(m_hi[:, t, :], p2_bank(t, at)[:, 0:D], ACT.Copy, scale=binv[1 - par][:, t:t + 1]).then_inc(m2_hi_done, 1)
                    if not is_m and live(at, 0):
                        nc.scalar.activation(squares[t], h[:, t, :], ACT.Square, bias=h_neg_mean[:, t:t + 1],
                                             accum_out=h_sq[:, t:t + 1]).then_inc(sq_done, 1)
                if at == 0:
                    act.wait_ge(scales_done, 2)
                    nc.scalar.activation(w2_hi[:, :, :], w2g_raw, ACT.Copy, scale=w_mul[:, 1:2]).then_inc(w2_hi_done, 1)
                if live(at, 0):
                    act.wait_ge(h_shift_done, n + 1)
                    for t in range(2):
                        nc.scalar.activation(h[:, t, :], h[:, t, :], ACT.Identity,
                                             bias=h_shift[:, t:t + 1], scale=h_rstd[:, t:t + 1]).then_inc(h_done, 1)

            run_steps(act, step)

            act.wait_ge(ffn_scales_done, 1)

            def magnitude(g, par, first):
                if not first:
                    act.wait_ge(q_rounder_done, g - 1)
                nc.scalar.activation(q_abs[par], v[:, bass.ds(g, 1), :, :].rearrange("p g k d -> p (g k d)"), ACT.Abs,
                                     scale=ffn_scale[:, 4:5]).then_inc(q_abs_done, 1)

            magnitude(0, 0, True)
            magnitude(1, 1, True)
            magnitude(2, 0, False)

            def ffn_step(n, par, at):
                if live(at, 3):
                    magnitude(n + 3, 1 - par, False)
                if live(at, 0):
                    act.wait_ge(qT_psum, PAIRS * (n + 1))
                    wait(act, y_psum, PAIRS * (n - 1))
                    nc.scalar.activation(qT[par], qT_banks[par][:, :].bitcast(BF16).rearrange("p (k c) -> p k c", k=DT),
                                         ACT.Copy).then_inc(qT_done, 1)

            run_ffn_steps(act, ffn_step)

        @block.vector
        def _(dve):
            chain = [0]

            def link(ins, k=1):
                chain[0] += k
                ins.then_inc(setup_vec, 1)
                dve.wait_ge(setup_vec, chain[0])

            nc.vector.memset(edge_rows, 0.0).then_inc(edge_rows_zero, 1)
            nc.vector.memset(edge_w[:, :, :, :], 0.0).then_inc(edge_rows_zero, 1)
            dve.wait_ge(ident_done, 1)
            nc.vector.tensor_copy(ident16[:, :], ident[:, :]).then_inc(ident16_done, 1)
            nc.vector.tensor_copy(ident_bf[:, :], ident[:, :]).then_inc(ident16_done, 1)

            def x_statistics(g):
                dve.wait_ge(x_in, 16 * (g + 1))
                nc.vector.memset(dve_gate[:, 0:1], 0.0)
                for t in range(TILES):
                    nc.vector.bn_stats(x_six[:, t, :], x1[:, bass.ds(g, 1), t, :].rearrange("p g d -> p (g d)")).then_inc(x_six_done, 1)
                dve.wait_ge(x_six_done, TILES * (g + 1))
                nc.vector.memset(dve_gate[:, 1:2], 0.0)
                for t in range(TILES):
                    ins = nc.vector.bn_aggr(x_mv[:, t, :], x_six[:, t, :])
                ins.then_inc(x_moments, 1)

            def make_u(g):
                dve.wait_ge(x_rstd_done, g + 1)
                wait(dve, base_done, g)
                for t in range(TILES):
                    nc.vector.tensor_scalar(u[:, t, :], x1[:, bass.ds(g, 1), t, :].rearrange("p g d -> p (g d)"),
                                            x_mv[:, t, 0:1], x_rstd[:, t:t + 1], ALU.subtract, ALU.mult).then_inc(u_done, 1)

            def make_mask(g, par):
                dve.wait_ge(adj_fetched, 16 * (g + 1))
                nc.vector.tensor_scalar(H[par][:, :, :], adj_in[:, :, :], 0.0, None, ALU.not_equal).then_inc(H_done, 1)

            x_statistics(0)
            make_u(0)
            make_mask(0, 0)

            dve.wait_ge(edge_rows_T, 1)
            edge_psum = bank[2][:, :].rearrange("p (k c) -> p k c", k=TILES)[:, :, 0:G]
            link(nc.vector.tensor_copy(edge_cols, edge_psum))
            nc.vector.tensor_copy(edge_w[:, :, :, 0], edge_cols).then_inc(edge_w_done, 1)
            dve.wait_ge(edge_w_done, 1)
            link(nc.vector.tensor_tensor(edge_rest, edge_cols, edge_w[:, :, :, 0], ALU.subtract))
            nc.vector.tensor_copy(edge_w[:, :, :, 1], edge_rest).then_inc(edge_w_done, 1)
            dve.wait_ge(edge_w_done, 2)
            link(nc.vector.tensor_tensor(edge_rest2, edge_rest, edge_w[:, :, :, 1], ALU.subtract))
            nc.vector.tensor_copy(edge_w[:, :, :, 2], edge_rest2).then_inc(edge_w_done, 1)

            dve.wait_ge(w1_in, 16)
            nc.vector.tensor_reduce(w_amax[:, 0:1], w1_raw, AX.XY, ALU.max, apply_absolute_value=True).then_inc(amax_rows, 1)

            def scale_w1():
                dve.wait_ge(amax_all, 1)
                link(nc.vector.tensor_scalar(w_safe[:, 0:1], w_amax_all[:, 0:1], WEIGHT_FLOOR, None, ALU.max))
                link(nc.vector.tensor_scalar(w_pow2[:, 0:1].bitcast(U32), w_safe[:, 0:1].bitcast(U32), EXPONENT, None, ALU.bitwise_and))
                link(nc.vector.reciprocal(w_inv[:, 0:1], w_pow2[:, 0:1]))
                nc.vector.tensor_scalar(w_mul[:, 0:1], w_inv[:, 0:1], W_SCALE, None, ALU.mult).then_inc(scales_done, 1)
                link(nc.vector.tensor_scalar(dinv_mul[:, 0:1], w_pow2[:, 0:1], 1.0 / (Z_SCALE * W_SCALE), None, ALU.mult))

            def magnitudes():
                dve.wait_ge(ffn_in, 16)
                nc.vector.tensor_reduce(w_amax[:, 3:4], ffn_raw, AX.X, ALU.max, apply_absolute_value=True).then_inc(amax_rows, 1)
                dve.wait_ge(w2g_done, 1)
                nc.vector.tensor_reduce(w_amax[:, 1:2], w2g_raw, AX.XY, ALU.max, apply_absolute_value=True).then_inc(amax_rows, 1)
                dve.wait_ge(bias_col_done, 1)
                link(nc.vector.tensor_reduce(w_amax[:, 2:3], bias_col[:, :], AX.X, ALU.max, apply_absolute_value=True))
                nc.vector.tensor_scalar(w_amax[:, 2:3], w_amax[:, 2:3], 1.0 / F, None, ALU.mult).then_inc(amax_rows, 1)

            def scale_w2():
                dve.wait_ge(amax_all, 2)
                link(nc.vector.tensor_tensor(w_safe[:, 1:2], w_amax_all[:, 1:2], w_amax_all[:, 2:3], ALU.max))
                link(nc.vector.tensor_scalar(w_safe[:, 1:2], w_safe[:, 1:2], WEIGHT_FLOOR, None, ALU.max))
                link(nc.vector.tensor_scalar(w_pow2[:, 1:2].bitcast(U32), w_safe[:, 1:2].bitcast(U32), EXPONENT, None, ALU.bitwise_and))
                link(nc.vector.reciprocal(w_inv[:, 1:2], w_pow2[:, 1:2]))
                nc.vector.tensor_scalar(w_mul[:, 1:2], w_inv[:, 1:2], W_SCALE, None, ALU.mult).then_inc(scales_done, 1)
                nc.vector.tensor_scalar(bias_mul[:, :], w_inv[:, 1:2], X_SCALE, None, ALU.mult)
                link(nc.vector.tensor_scalar(dinv_mul[:, 1:2], w_pow2[:, 1:2], 1.0 / X_SCALE, None, ALU.mult))
                nc.vector.tensor_scalar(dinv2[0][:, :], dinv[:, :], dinv_mul[:, 1:2], None, ALU.mult).then_inc(dinv2_done, 1)

            def finish_w2():
                dve.wait_ge(w2_hi_done, 1)
                nc.vector.scalar_tensor_tensor(w2_lo[:, :, :], w2g_raw, w_mul[:, 1:2], w2_hi[:, :, :],
                                               ALU.mult, ALU.subtract).then_inc(weights_done, 1)
                dve.wait_ge(bias_T, 1)
                nc.vector.tensor_scalar(beta_w2[:, :], bank[6][:, D:2 * D], bias_mul[:, :], None, ALU.mult).then_inc(bias_out, 1)
                dve.wait_ge(bias_out, 1)

            def round_ffn_weight():
                link(nc.vector.tensor_scalar(w_safe[:, 3:4], w_amax_all[:, 3:4], AMAX_FLOOR, None, ALU.max))
                link(nc.vector.reciprocal(w_inv[:, 3:4], w_safe[:, 3:4]))
                link(nc.vector.tensor_scalar(w_mul[:, 3:4], w_inv[:, 3:4], FP8_MAX, None, ALU.mult))
                link(nc.vector.reciprocal(ffn_scale[:, 6:7], w_mul[:, 3:4]))
                link(nc.vector.tensor_scalar(wq_in, ffn_raw, w_mul[:, 3:4], None, ALU.mult))
                link(nc.vector.scalar_tensor_tensor(wq_rounder, wq_in, -1.0, wq_in, ALU.mult, ALU.max))
                link(nc.vector.tensor_scalar(wq_rounder, wq_rounder, ROUND_FLOOR, ROUND_SCALE, ALU.max, ALU.mult))
                link(nc.vector.tensor_tensor(wq_sum, wq_in, wq_rounder, ALU.add))
                link(nc.vector.tensor_tensor(wq[:, :, :].rearrange("p k d -> p (k d)"), wq_sum, wq_rounder, ALU.subtract))

            def step(n, par, at):
                def maskT_out(j):
                    dve.wait_ge(HT_psum, 2 * n + j + 1)
                    nc.vector.tensor_copy(HT[par][:, 2 * j:2 * j + 2, :].rearrange("p a c -> p (a c)"),
                                          ht_banks[j][:, :].bitcast(FP16)).then_inc(HT_done, 1)

                def m_low(j):
                    dve.wait_ge(m_hi_done, TILES * n + j + 1)
                    nc.vector.scalar_tensor_tensor(m_lo[:, j, :], p_bank(j, at)[:, 0:D], binv64[:, j:j + 1], m_hi[:, j, :],
                                                   ALU.mult, ALU.subtract).then_inc(m_lo_done, 1)

                def h_low(t):
                    dve.wait_ge(hT_hi_done, TILES * (n - 1) + t + 1)
                    nc.vector.tensor_tensor(hT_lo[:, t, :], t_bank(t, at)[:, :], hT_hi[:, t, :], ALU.subtract).then_inc(hT_lo_done, 1)

                def invert_count(j):
                    dve.wait_ge(p_psum, TILES * n + j + 1)
                    nc.vector.tensor_scalar(count64[:, j:j + 1], p_bank(j, at)[:, D:D + 1], 1.0, 1.0 / M_SCALE, ALU.max, ALU.mult).then_inc(dve_chain, 1)
                    dve.wait_ge(dve_chain, 5 * n + j + 1)
                    nc.vector.reciprocal(binv64[:, j:j + 1], count64[:, j:j + 1]).then_inc(binv_done, 1)

                order = ((maskT_out, 0), (invert_count, 0), (invert_count, 1), (m_low, 0), (invert_count, 2), (m_low, 1), (m_low, 2),
                         (h_low, 0), (invert_count, 3), (maskT_out, 1), (m_low, 3), (h_low, 1), (h_low, 2), (h_low, 3))
                if at == 1:
                    order = ((maskT_out, 0), (maskT_out, 1), *((work, j) for work in (invert_count, m_low, h_low) for j in range(TILES)))
                for work, j in order:
                    if live(at, -1 if work is h_low else 0):
                        work(j)
                    if at == 0 and (work, j) == (maskT_out, 0):
                        scale_w1()
                if at == 1:
                    finish_w2()
                if live(at, 0):
                    dve.wait_ge(binv_done, TILES * (n + 1))
                    nc.vector.tensor_scalar(binv[par][:, :], binv64[:, :], 1.0 / M_SCALE, None, ALU.mult).then_inc(dve_chain, 1)
                if live(at, -2):
                    nc.vector.bn_stats(v_six[:, TILES - 1, :], x1[:, bass.ds(n - 2, 1), TILES - 1, :].rearrange("p g d -> p (g d)")).then_inc(v_six_done, 1)
                    dve.wait_ge(v_six_done, TILES * (n - 1))
                    nc.vector.memset(dve_gate[:, 2:3], 0.0)
                    for t in range(TILES):
                        ins = nc.vector.bn_aggr(v_mv[:, t, :], v_six[:, t, :])
                    ins.then_inc(v_moments, 1)
                if at == G + 1:
                    round_ffn_weight()
                if live(at, 1) and at != 0:
                    x_statistics(n + 1)
                if at == 0:
                    for k in range(DT):
                        dve.wait_ge(w1_hi_done, k + 1)
                        nc.vector.scalar_tensor_tensor(w1_lo[:, k, :], w1T_raw[:, k, :], w_mul[:, 0:1], w1_hi[:, k, :],
                                                       ALU.mult, ALU.subtract).then_inc(weights_done, 1)
                if live(at, 0):
                    for k in range(DT):
                        dve.wait_ge(z_hi_done, DT * n + k + 1)
                        nc.vector.scalar_tensor_tensor(z_lo[:, k, :], z_banks[k][:, :], Z_DOWN, z_hi[:, k, :],
                                                       ALU.mult, ALU.subtract).then_inc(z_lo_done, 1)
                        if at == 0 and k == 0:
                            make_mask(1, 1)

                def add_beta_w2(q):
                    dve.wait_ge(xw_psum, PAIRS * (n - 1) + q + 1)
                    nc.vector.scalar_tensor_tensor(xw[q].rearrange("p (a d) -> p a d", a=2), x_banks[q][:, :].rearrange("p (a d) -> p a d", a=2), X_DOWN,
                                                   beta_w2[:, :].unsqueeze(1).to_broadcast([PART, 2, D]), ALU.mult, ALU.add).then_inc(xw_done, 1)

                if live(at, -1):
                    add_beta_w2(0)
                if live(at, 1) and at != 0:
                    make_u(n + 1)
                if live(at, 0):
                    dve.wait_ge(d_psum, n + 1)
                    nc.vector.tensor_reduce(deg[:, :], d_bank[:, 0:TILES * W_PAD].rearrange("p (k c) -> p k c", c=W_PAD), AX.X, ALU.add).then_inc(deg_steps, 1)
                    dve.wait_ge(deg_steps, 4 * n + 1)
                    nc.vector.tensor_scalar(deg_pos[:, :], deg[:, :], 0.0, None, ALU.is_gt)
                    nc.vector.tensor_scalar(deg_safe[:, :], deg[:, :], SMALLEST, None, ALU.max).then_inc(deg_steps, 1)
                    dve.wait_ge(deg_steps, 4 * n + 2)
                    nc.vector.reciprocal(deg_inv[:, :], deg_safe[:, :]).then_inc(deg_steps, 1)
                    dve.wait_ge(deg_steps, 4 * n + 3)
                    nc.vector.tensor_tensor(dinv[:, :], deg_inv[:, :], deg_pos[:, :], ALU.mult).then_inc(deg_steps, 1)
                    dve.wait_ge(deg_steps, 4 * n + 4)
                    nc.vector.tensor_scalar(dinv1[:, :], dinv[:, :], dinv_mul[:, 0:1], None, ALU.mult).then_inc(dinv1_done, 1)
                    if at != 0:
                        nc.vector.tensor_scalar(dinv2[par][:, :], dinv[:, :], dinv_mul[:, 1:2], None, ALU.mult).then_inc(dinv2_done, 1)
                if live(at, -1):
                    add_beta_w2(1)
                if at == G + 1:
                    for q in range(PAIRS):
                        dve.wait_ge(v_done, TILES * (n - 2) + 2 * (q + 1))
                        nc.vector.tensor_reduce(v_amax[:, n - 2 + q:n - 1 + q], v[:, n - 2, 2 * q:2 * q + 2, :], AX.XY, ALU.max, apply_absolute_value=True).then_inc(v_amax_done, 1)
                elif live(at, -2):
                    dve.wait_ge(v_done, TILES * (n - 1))
                    nc.vector.tensor_reduce(v_amax[:, bass.ds(n - 2, 1)], v[:, bass.ds(n - 2, 1), :, :].rearrange("p g k d -> p (g k) d"), AX.XY, ALU.max, apply_absolute_value=True).then_inc(v_amax_done, 1)
                if at == 0:
                    x_statistics(1)
                if live(at, 0):
                    dve.wait_ge(dinv1_done, n + 1)
                    if at == 0:
                        dve.wait_ge(vec_in, 64)
                    for t in range(TILES):
                        if at == 0 and t == 2:
                            make_u(1)
                        dve.wait_ge(a_psum, TILES * n + t + 1)
                        nc.vector.scalar_tensor_tensor(h[:, t, :], a_banks[t][:, :], dinv1[:, t:t + 1], b1_all[:, :],
                                                       ALU.mult, ALU.add).then_inc(a_done, 1)
                    dve.wait_ge(relu_done, TILES * (n + 1))
                    nc.vector.tensor_scalar(h_neg_mean[:, :], h_sum[:, :], -1.0 / F, None, ALU.mult).then_inc(mean_done, 1)
                if at == 0:
                    dve.wait_ge(bias_col_psum, 1)
                    nc.vector.tensor_copy(bias_col[:, :], bank[5][:, 0:DT]).then_inc(bias_col_done, 1)
                if live(at, -1):
                    for t in range(TILES):
                        dve.wait_ge(m2_hi_done, TILES * (n - 1) + t + 1)
                        nc.vector.scalar_tensor_tensor(m_lo[:, t, :], p2_bank(t, at)[:, 0:D], binv[1 - par][:, t:t + 1], m_hi[:, t, :],
                                                       ALU.mult, ALU.subtract).then_inc(m2_lo_done, 1)
                if live(at, 1) and at != 0:
                    make_mask(n + 1, 1 - par)
                if at == 0:
                    magnitudes()
                    scale_w2()
                if live(at, -1):
                    dve.wait_ge(base_done, n)
                    dve.wait_ge(dinv2_done, n)
                    row = [x1[:, bass.ds(n - 1, 1), t, :].rearrange("p g d -> p (g d)") for t in range(TILES)]
                    for t in range(TILES):
                        if t >= 1:
                            dve.wait_ge(x1_done, TILES * (n - 1) + t)
                        dve.wait_ge(o_psum, TILES * (n - 1) + t + 1)
                        nc.vector.scalar_tensor_tensor(row[t], o_banks[t][:, 0:D], dinv2[1 - par][:, t:t + 1], row[t],
                                                       ALU.mult, ALU.add).then_inc(x1_done, 1)
                        if t >= 1:
                            nc.vector.bn_stats(v_six[:, t - 1, :], row[t - 1]).then_inc(v_six_done, 1)
                    dve.wait_ge(x1_done, TILES * n)
                    nc.vector.memset(dve_gate[:, 3:4], 0.0)

            run_steps(dve, step)

            dve.wait_ge(v_amax_done, G + 1)
            nc.vector.tensor_reduce(ffn_scale[:, 0:1], v_amax[:, :], AX.X, ALU.max).then_inc(row_amax_done, 1)
            dve.wait_ge(all_amax_done, 1)
            link(nc.vector.tensor_scalar(ffn_scale[:, 2:3], ffn_scale[:, 1:2], AMAX_FLOOR, None, ALU.max))
            link(nc.vector.reciprocal(ffn_scale[:, 3:4], ffn_scale[:, 2:3]))
            nc.vector.tensor_scalar(ffn_scale[:, 4:5], ffn_scale[:, 3:4], FP8_MAX, None, ALU.mult).then_inc(ffn_scales_done, 1)
            dve.wait_ge(ffn_scales_done, 1)
            link(nc.vector.reciprocal(ffn_scale[:, 5:6], ffn_scale[:, 4:5]))
            link(nc.vector.tensor_tensor(ffn_scale[:, 7:8], ffn_scale[:, 5:6], ffn_scale[:, 6:7], ALU.mult))

            def rounder(g, par):
                dve.wait_ge(q_abs_done, g + 1)
                nc.vector.tensor_scalar(q_rounder[par], q_abs[par], ROUND_FLOOR, ROUND_SCALE, ALU.max, ALU.mult).then_inc(q_rounder_done, 1)

            rounder(0, 0)

            def ffn_step(n, par, at):
                if live(at, 0):
                    dve.wait_ge(q_rounder_done, n + 1)
                    nc.vector.scalar_tensor_tensor(q_sum[par], v[:, bass.ds(n, 1), :, :].rearrange("p g k d -> p (g k d)"), ffn_scale[:, 4:5],
                                                   q_rounder[par], ALU.mult, ALU.add).then_inc(q_sum_done, 1)
                if live(at, 1) and at != 0:
                    wait_q(dve, n - 1, None if at is None else at - 1)
                if live(at, 1):
                    rounder(n + 1, 1 - par)
                if at in Q_ENDS:
                    wait(dve, qT_psum, PAIRS * (n - 1))
                    dve.wait_ge(q_sum_done, n + 1)
                    for half in range(PAIRS):
                        part = slice(2 * D * half, 2 * D * (half + 1))
                        nc.vector.tensor_tensor(q_nat[par][:, part], q_sum[par][:, part], q_rounder[par][:, part], ALU.subtract).then_inc(q_ends_done, 1)
                if live(at, -2):
                    for q in range(PAIRS):
                        dve.wait_ge(y_psum, PAIRS * (n - 2) + q + 1)
                        row = x1[:, bass.ds(n - 2, 1), 2 * q:2 * q + 2, :].rearrange("p g k d -> p (g k d)")
                        nc.vector.scalar_tensor_tensor(row, y_banks[par][q][:, :], ffn_scale[:, 7:8], row,
                                                       ALU.mult, ALU.add).then_inc(y_done, 1)

            run_ffn_steps(dve, ffn_step)

        @block.tensor
        def _(pe):
            pe.wait_ge(ident_done, 1)
            pe.wait_ge(edge_in, 16)
            for k in range(TILES):
                ins = nc.tensor.transpose(bank[2][:, PART * k:PART * (k + 1)], edge_rows[:, PART * k:PART * (k + 1)], ident[:, :])
            ins.then_inc(edge_rows_T, 1)
            pe.wait_ge(w1_in, 16)
            for k in range(DT):
                for f in range(FT):
                    ins = nc.tensor.transpose(bank[3 + k][:, PART * f:PART * (f + 1)], w1_raw[:, f, PART * k:PART * (k + 1)], ident[:, :])
                ins.then_inc(w1_T, 1)
            pe.wait_ge(ident16_done, 2)
            pe.wait_ge(consts_done, 4)

            def step(n, par, at):
                mask, maskT, old_mask, old_maskT = H[par], HT[par], H[1 - par], HT[1 - par]
                if live(at, 0):
                    pe.wait_ge(H_done, n + 1)
                    wait(pe, deg_steps, 4 * n - 3)
                    for j in range(2):
                        for e in range(2):
                            for t in range(TILES):
                                ins = nc.tensor.transpose(
                                    ht_banks[j][:, :].bitcast(FP16)[:, C * e + PART * t:C * e + PART * (t + 1)],
                                    mask[:, t, PART * (2 * j + e):PART * (2 * j + e + 1)], ident16[:, :])
                        ins.then_inc(HT_psum, 1)
                    pe.wait_ge(u_lo_done, n + 1)

                def edge_sums(j):
                    if at == 0 and j == 2:
                        pe.wait_ge(edge_w_done, 3)
                    if j < 3:
                        wait(pe, x1_done, TILES * (n - 2) + j + 2)
                    elif at == 1:
                        pe.wait_ge(HT_done, 2 * (n + 1))
                    else:
                        pe.wait_ge(m_lo_done, TILES * n + 1)
                    for k in range(TILES):
                        nc.tensor.matmul(p_bank(j, at)[:, 0:D + 1], mask[:, k, PART * j:PART * (j + 1)], u_hi[:, k, 0:D + 1],
                                         start=(k == 0), stop=False)
                        ins = nc.tensor.matmul(p_bank(j, at)[:, 0:D], mask[:, k, PART * j:PART * (j + 1)], u_lo[:, k, :],
                                               start=False, stop=(k == TILES - 1))
                    ins.then_inc(p_psum, 1)

                def spread_bias():
                    pe.wait_ge(bias_col_done, 1)
                    for o in range(DT):
                        ins = nc.tensor.matmul(bank[6][:, D + PART * o:D + PART * (o + 1)], bias_col[:, o:o + 1].to_broadcast([PART, PART]),
                                               ident[:, :], start=True, stop=True)
                    ins.then_inc(bias_T, 1)

                def transpose_h(t):
                    pe.wait_ge((h_done, h_done_pool)[t // 2], 2 * (n - 1) + t % 2 + 1)
                    if t == 2:
                        wait(pe, x1_done, TILES * (n - 2) + 1)
                    if t == 3 and at == 1:
                        pe.wait_ge(m_lo_done, TILES * n + 1)
                    elif t == 3 and live(at, 0):
                        pe.wait_ge(HT_done, 2 * n + 1)
                    for k in range(FT):
                        ins = nc.tensor.transpose(t_bank(t, at)[:, PART * k:PART * (k + 1)], h[:, t, PART * k:PART * (k + 1)], ident[:, :])
                    ins.then_inc(hT_psum, 1)

                for is_m, tiles in first_order(at):
                    for j in tiles:
                        if is_m and live(at, 0):
                            edge_sums(j)
                            if (at, j) == (1, 3):
                                spread_bias()
                        if not is_m and live(at, -1):
                            transpose_h(j)
                if live(at, 0):
                    pe.wait_ge(HT_done, 2 * n + 1)
                    if at == 0:
                        pe.wait_ge(w1T_copied, DT)
                    for d in range(DT):
                        wait(pe, hT_lo_done, TILES * (n - 1) + 1 + d)
                        for k in range(TILES):
                            if d == 0:
                                pe.wait_ge(m_lo_done, TILES * n + k + 1)
                                if k == 2:
                                    pe.wait_ge(HT_done, 2 * (n + 1))
                            nc.tensor.matmul(z_banks[d][:, :], m_hi[:, k, PART * d:PART * (d + 1)], maskT[:, k, :], start=(k == 0), stop=False)
                            ins = nc.tensor.matmul(z_banks[d][:, :], m_lo[:, k, PART * d:PART * (d + 1)], maskT[:, k, :],
                                                   start=False, stop=(k == TILES - 1))
                        ins.then_inc(z_psum, 1)
                    pe.wait_ge(edge_w_copied, n + 1)
                    wait(pe, hT_lo_done, TILES * n)
                    if at == 1:
                        pe.wait_ge(bias_out, 1)
                    for t in range(TILES):
                        for k in range(TILES):
                            ins = nc.tensor.matmul(d_bank[:, W_PAD * t:W_PAD * (t + 1)], maskT[:, k, PART * t:PART * (t + 1)],
                                                   edge_w_now[:, k, :], start=(k == 0), stop=(k == TILES - 1))
                    ins.then_inc(d_psum, 1)
                if at == 0:
                    pe.wait_ge(w2_in, 16)
                    for q in range(PAIRS):
                        pe.wait_ge(m_lo_done, q + 2)
                        for kk in range(2):
                            for o in range(DT):
                                f = 2 * q + kk
                                ins = nc.tensor.transpose(bank[1 + q][:, D * kk + PART * o:D * kk + PART * (o + 1)],
                                                          w2_raw[:, o, PART * f:PART * (f + 1)], ident[:, :])
                        ins.then_inc(w2_T, 1)
                if live(at, -1):
                    if at == 1:
                        pe.wait_ge(weights_done, DT + 1)
                    for q in range(PAIRS):
                        pe.wait_ge(hT_lo_done, TILES * (n - 1) + 3 + q)
                        if q == 1 and live(at, 0):
                            pe.wait_ge(z_lo_done, DT * n + 1)
                        for tt in range(2):
                            t = 2 * q + tt
                            for k in range(FT):
                                dst = x_banks[q][:, D * tt:D * (tt + 1)]
                                hi, lo = hT_hi[:, t, PART * k:PART * (k + 1)], hT_lo[:, t, PART * k:PART * (k + 1)]
                                nc.tensor.matmul(dst, hi, w2_hi[:, k, :], start=(k == 0), stop=False)
                                nc.tensor.matmul(dst, hi, w2_lo[:, k, :], start=False, stop=False)
                                ins = nc.tensor.matmul(dst, lo, w2_hi[:, k, :], start=False, stop=(k == FT - 1))
                        ins.then_inc(xw_psum, 1)
                if live(at, 0):
                    if at == 0:
                        pe.wait_ge(weights_done, DT)
                    pe.wait_ge(z_lo_done, DT * (n + 1))
                    for t in range(TILES):
                        if t in (1, 2):
                            wait(pe, xw_done, PAIRS * (n - 1) + t)
                        if t == 3:
                            pe.wait_ge(a_done, TILES * n + 1)
                        for k in range(DT):
                            hi, lo = z_hi[:, k, PART * t:PART * (t + 1)], z_lo[:, k, PART * t:PART * (t + 1)]
                            nc.tensor.matmul(a_banks[t][:, :], hi, w1_hi[:, k, :], start=(k == 0), stop=False)
                            nc.tensor.matmul(a_banks[t][:, :], hi, w1_lo[:, k, :], start=False, stop=False)
                            ins = nc.tensor.matmul(a_banks[t][:, :], lo, w1_hi[:, k, :], start=False, stop=(k == DT - 1))
                        ins.then_inc(a_psum, 1)
                if at == 0:
                    pe.wait_ge(vec_in, 64)
                    pe.wait_ge(w2T_copied, PAIRS)
                    pe.wait_ge(a_done, 2)
                    for o in range(DT):
                        for f in range(FT):
                            ins = nc.tensor.matmul(bank[5][:, o:o + 1], w2T_raw[:, f, PART * o:PART * (o + 1)], beta_col[:, f:f + 1],
                                                   start=(f == 0), stop=(f == FT - 1))
                    ins.then_inc(bias_col_psum, 1)
                if live(at, -1):
                    for halves in ((0, 1), (2, 3)) if at == G else ((0, 1, 2, 3),):
                        pe.wait_ge(xw_lo_done, PAIRS * (n - 1) + (halves[-1] + 1) // 2)
                        for j in range(TILES):
                            if j < 3:
                                if live(at, 0):
                                    pe.wait_ge(m_lo_done, TILES * n + j + 2)
                                else:
                                    pe.wait_ge(x1_done, TILES * (n - 1))
                            elif live(at, 0):
                                pe.wait_ge(m2_lo_done, TILES * (n - 1) + 1)
                            for k in halves:
                                nc.tensor.matmul(p2_bank(j, at)[:, 0:D], old_mask[:, k, PART * j:PART * (j + 1)], xw_hi[:, k, :], start=(k == 0), stop=False)
                                ins = nc.tensor.matmul(p2_bank(j, at)[:, 0:D], old_mask[:, k, PART * j:PART * (j + 1)], xw_lo[:, k, :],
                                                       start=False, stop=(k == TILES - 1))
                            if k == TILES - 1:
                                ins.then_inc(p2_psum, 1)
                if live(at, -1):
                    if live(at, 0):
                        pe.wait_ge(a_done, TILES * n + 2)
                    for k in range(TILES):
                        pe.wait_ge(m2_lo_done, TILES * (n - 1) + k + 1)
                        for t in (range(1) if k < 2 else range(2)):
                            for kk in (range(3) if (t, k) == (1, 2) else (k,)):
                                nc.tensor.matmul(o_banks[t][:, 0:D], old_maskT[:, kk, PART * t:PART * (t + 1)], m_hi[:, kk, :], start=(kk == 0), stop=False)
                                ins = nc.tensor.matmul(o_banks[t][:, 0:D], old_maskT[:, kk, PART * t:PART * (t + 1)], m_lo[:, kk, :],
                                                       start=False, stop=(kk == TILES - 1))
                            if k == TILES - 1:
                                ins.then_inc(o_psum, 1)
                    for t in (2, 3):
                        for k in range(TILES):
                            nc.tensor.matmul(o_banks[t][:, 0:D], old_maskT[:, k, PART * t:PART * (t + 1)], m_hi[:, k, :], start=(k == 0), stop=False)
                            ins = nc.tensor.matmul(o_banks[t][:, 0:D], old_maskT[:, k, PART * t:PART * (t + 1)], m_lo[:, k, :],
                                                   start=False, stop=(k == TILES - 1))
                        ins.then_inc(o_psum, 1)

            run_steps(pe, step)

            def transpose_q(g, par, at, half):
                wait_q(pe, g, at, half)
                for t in (2 * half, 2 * half + 1):
                    for k in range(DT):
                        ins = nc.tensor.transpose(qT_banks[par][:, :].bitcast(BF16)[:, C * k + PART * t:C * k + PART * (t + 1)],
                                                  q_nat[par][:, D * t + PART * k:D * t + PART * (k + 1)], ident_bf[:, :])
                ins.then_inc(qT_psum, 1)

            def ffn_step(n, par, at):
                for q in range(PAIRS):
                    if live(at, 1):
                        transpose_q(n + 1, 1 - par, None if at is None else at + 1, q)
                    if live(at, 0):
                        pe.wait_ge(qT_done, n + 1)
                        wait(pe, y_done, PAIRS * (n - 2) + q + 1)
                        for tt in range(2):
                            t = 2 * q + tt
                            for k in range(DT):
                                ins = nc.tensor.matmul(y_banks[par][q][:, D * tt:D * (tt + 1)], qT[par][:, k, PART * t:PART * (t + 1)], wq[:, k, :],
                                                       start=(k == 0), stop=(k == DT - 1))
                        ins.then_inc(y_psum, 1)

            pe.wait_ge(x1_done, TILES * G)
            for half in range(PAIRS):
                transpose_q(0, 0, 0, half)
            run_ffn_steps(pe, ffn_step)


_INS = ["x", "adj", "L0_gnn_W1", "L0_gnn_b1", "L0_gnn_gamma", "L0_gnn_beta", "L0_gnn_W2", "L0_gnn_b2", "L0_ffn_weight"]


def kernel(**inputs):
    import numpy as _np
    import concourse.bacc as _bacc
    from concourse import mybir as _mybir
    from concourse.bass_utils import run_bass_kernel_spmd as _run

    nc = _bacc.Bacc("TRN2", target_bir_lowering=False, num_devices=1)
    arrays, args = {}, []
    for name in _INS:
        a = _np.ascontiguousarray(inputs[name])
        arrays[f"in_{name}_dram"] = a
        args.append(nc.dram_tensor(f"in_{name}_dram", a.shape, _mybir.dt.from_np(a.dtype), kind="ExternalInput").ap())
    shape = arrays["in_x_dram"].shape
    args.append(nc.dram_tensor("out_0_dram", shape, _mybir.dt.float32, kind="ExternalOutput").ap())
    adjacency_gnn_then_fp8_ffn(nc, *args)
    r = _run(nc, [arrays], core_ids=[0])
    return r.results[0]["out_0_dram"]
```
